# Optimizing a Trainium2 kernel written in Bass

```python
import numpy as np
import jax
import jax.numpy as jnp

def _softmax(x, axis=-1):
    return jax.nn.softmax(x, axis=axis)
def _gelu(x):
    return jax.nn.gelu(x, approximate=True)
def _silu(x):
    return jax.nn.silu(x)
def _sigmoid(x):
    return jax.nn.sigmoid(x)
def _layernorm(x, axis=-1, eps=1e-5):
    m = jnp.mean(x, axis=axis, keepdims=True)
    v = jnp.var(x, axis=axis, keepdims=True)
    return (x - m) / jnp.sqrt(v + eps)
def _scatter_add(tgt, idx, src, axis=0):
    return tgt.at[idx].add(src)
def _segment_sum(src, seg, n):
    return jax.ops.segment_sum(src, seg, n)

kernel_name = 'mk_adj_preln_d2_adj_512_f775d3'

def setup_inputs(seed: int = 0):
    np.random.seed(seed)
    _w = jnp.asarray
    def _rec_inputs():
        import jax
        import jax.numpy as jnp
        _gk = jax.random.key(seed)
        x = -0.001003 + 1 * jax.random.normal(jax.random.fold_in(_gk, 1), (4096, 512), jnp.float32)
        _a = jax.random.bernoulli(jax.random.fold_in(_gk, 2), 0.0078125, (4096, 4096))
        _a = jnp.logical_or(_a, jnp.swapaxes(_a, -1, -2))
        _a = jnp.logical_or(_a, jnp.eye(4096, dtype=bool))
        adj = _a.astype(jnp.int32)
        return x, adj
    x, adj = _rec_inputs()
    def _L0_gnn_setup():
        import jax, jax.numpy as jnp
        import numpy as np
        N, IN_F, H, D = (3072, 512, 8, 64)
        key = jax.random.key(seed)
        k1, k2, k3, k4, k5 = jax.random.split(key, 5)
        x = jax.random.normal(k1, (N, IN_F), dtype=jnp.float32)
        adj = jax.random.randint(k2, (N, N), 0, 2, dtype=jnp.int32)
        s_W = (6.0 / (IN_F + H * D)) ** 0.5
        s_a = (6.0 / (H + D)) ** 0.5
        W = jax.random.uniform(k3, (H * D, IN_F), dtype=jnp.float32, minval=-s_W, maxval=s_W)
        a_src = jax.random.uniform(k4, (H, D), dtype=jnp.float32, minval=-s_a, maxval=s_a)
        a_dst = jax.random.uniform(k5, (H, D), dtype=jnp.float32, minval=-s_a, maxval=s_a)
        return {'x': x, 'adj': adj, 'W': W, 'a_src': a_src, 'a_dst': a_dst}
    _L0_gnn_all = _L0_gnn_setup()
    _L0_gnn_in = {k: v for k, v in _L0_gnn_all.items() if k in ('W', 'a_src', 'a_dst', )}
    del _L0_gnn_all

    def _L1_gnn_setup():
        import jax, jax.numpy as jnp
        import numpy as np
        N, D_IN, D_OUT = (8192, 512, 512)
        key = jax.random.key(seed)
        ks = jax.random.split(key, 8)
        scale_in = 1.0 / np.sqrt(D_IN)
        scale_cat = 1.0 / np.sqrt(2 * D_OUT)
        return {'x': jax.random.normal(ks[0], (N, D_IN), dtype=jnp.float32), 'adj': jax.random.randint(ks[1], (N, N), 0, 2, dtype=jnp.int32), 'W_self': jax.random.uniform(ks[2], (D_IN, D_OUT), jnp.float32, -scale_in, scale_in), 'b_self': jax.random.uniform(ks[3], (D_OUT,), jnp.float32, -scale_in, scale_in), 'W_nb': jax.random.uniform(ks[4], (D_IN, D_OUT), jnp.float32, -scale_in, scale_in), 'b_nb': jax.random.uniform(ks[5], (D_OUT,), jnp.float32, -scale_in, scale_in), 'W_comb': jax.random.uniform(ks[6], (2 * D_OUT, D_OUT), jnp.float32, -scale_cat, scale_cat), 'b_comb': jax.random.uniform(ks[7], (D_OUT,), jnp.float32, -scale_cat, scale_cat)}
    _L1_gnn_all = _L1_gnn_setup()
    _L1_gnn_in = {k: v for k, v in _L1_gnn_all.items() if k in ('W_self', 'b_self', 'W_nb', 'b_nb', 'W_comb', 'b_comb', )}
    del _L1_gnn_all

    return {
        "x": x,
        "adj": adj,
        "L0_gnn_W": _L0_gnn_in["W"],
        "L0_gnn_a_src": _L0_gnn_in["a_src"],
        "L0_gnn_a_dst": _L0_gnn_in["a_dst"],
        "L1_gnn_W_self": _L1_gnn_in["W_self"],
        "L1_gnn_b_self": _L1_gnn_in["b_self"],
        "L1_gnn_W_nb": _L1_gnn_in["W_nb"],
        "L1_gnn_b_nb": _L1_gnn_in["b_nb"],
        "L1_gnn_W_comb": _L1_gnn_in["W_comb"],
        "L1_gnn_b_comb": _L1_gnn_in["b_comb"],
    }

def reference(x, adj, L0_gnn_W, L0_gnn_a_src, L0_gnn_a_dst, L1_gnn_W_self, L1_gnn_b_self, L1_gnn_W_nb, L1_gnn_b_nb, L1_gnn_W_comb, L1_gnn_b_comb):
    import jax
    import jax.numpy as jnp
    def _L0_gnn_ref(x, adj, W, a_src, a_dst):
        import jax, jax.numpy as jnp
        import numpy as np
        N, IN_F, H, D = (3072, 512, 8, 64)
        n = x.shape[0]
        Hh, d = a_src.shape
        h = (x @ W.T).reshape(n, Hh, d)
        e_src = jnp.einsum('nhd,hd->nh', h, a_src)
        e_dst = jnp.einsum('nhd,hd->nh', h, a_dst)
        e = e_src[:, None, :] + e_dst[None, :, :]
        e = jax.nn.leaky_relu(e, negative_slope=0.2)
        mask = adj + jnp.eye(n, dtype=adj.dtype) > 0
        e = jnp.where(mask[:, :, None], e, -jnp.inf)
        alpha = jax.nn.softmax(e, axis=1)
        out = jnp.einsum('ijh,jhd->ihd', alpha, h)
        return out.reshape(n, Hh * d)

    def _L1_gnn_ref(x, adj, W_self, b_self, W_nb, b_nb, W_comb, b_comb):
        import jax, jax.numpy as jnp
        import numpy as np
        N, D_IN, D_OUT = (8192, 512, 512)
        mask = (adj > 0).astype(x.dtype)
        deg = jnp.sum(mask, axis=1, keepdims=True)
        agg = mask @ x / jnp.maximum(deg, 1.0)
        self_f = x @ W_self + b_self
        nb_f = agg @ W_nb + b_nb
        combined = jnp.concatenate([self_f, nb_f], axis=-1)
        out = combined @ W_comb + b_comb
        return jax.nn.relu(out)

    h = jnp.maximum(_layernorm(x, axis=-1), 0.0)
    x = x + _L0_gnn_ref(h, adj, L0_gnn_W, L0_gnn_a_src, L0_gnn_a_dst)
    h = jnp.maximum(_layernorm(x, axis=-1), 0.0)
    x = x + _L1_gnn_ref(h, adj, L1_gnn_W_self, L1_gnn_b_self, L1_gnn_W_nb, L1_gnn_b_nb, L1_gnn_W_comb, L1_gnn_b_comb)
    return x


_drawn_inputs = setup_inputs


def setup_inputs(seed=0):
    import zlib

    import numpy as np

    out = dict(_drawn_inputs(seed))
    spreads = {}
    factors = {'L0_gnn_a_src': 2.844, 'L1_gnn_b_self': 8.0, 'L1_gnn_b_nb': 8.0, 'L1_gnn_b_comb': 5.105}
    for name, (base, spread) in spreads.items():
        noise = np.random.default_rng([zlib.crc32(name.encode()), seed]).standard_normal(out[name].shape)
        drawn = base * np.exp(spread * noise) if base else spread * noise
        out[name] = jnp.asarray(drawn.astype(out[name].dtype))
    for name, factor in factors.items():
        out[name] = (out[name] * factor).astype(out[name].dtype)
    return out
```

```python
import concourse.bass as bass
from concourse import mybir
from contextlib import ExitStack

F32 = mybir.dt.float32
BF16 = mybir.dt.bfloat16
FP16 = mybir.dt.float16
I32 = mybir.dt.int32
ALU = mybir.AluOpType
ACT = mybir.ActivationFunctionType
AX = mybir.AxisListType
RMAX = bass.bass_isa.ReduceOp.max

P = 128
F = 512
FC = F // P
H = 8
D = F // H
DE = D + 1
PARTS = 3
VW = PARTS * DE
SLOPE = 0.2
EPS = 1e-5
BIG = float(2 ** 60)
IB = 1024
KB = IB // P
IB1 = 512
G = 4
BANKS = 8


def build(nc, x, adj, W, a_src, a_dst, W_self, b_self, W_nb, b_nb, W_comb, b_comb, out):
    N = x.shape[0]
    NT = N // P
    NB = N // IB
    NB1 = N // IB1
    NG = NT // G
    JQ = N // 4
    TQ = JQ // P
    TI = IB1 // P
    CB = TQ * TI * P // 1024

    def dram(name, shape, dt):
        return nc.dram_tensor(name, shape, dt, kind="Internal").ap()

    maskT = dram("maskT_dram", (N, N), BF16)
    diag_raw = dram("diag_dram", (P, NT, P), BF16)
    s_rows = dram("s_rows_dram", (NB, H, IB), F32)
    vals = dram("vals_dram", (H, P, NT, 2 * VW), BF16)
    attn = dram("attn_dram", (NB, H, P, KB * D), F32)
    x1_self = dram("x1_self_dram", (NT, P, 2, F), F32)
    wsc_dram = dram("wsc_dram", (P, 2 * FC * F + F), F32)

    whole = ExitStack()
    with whole:
        def sem(name):
            return whole.enter_context(nc.semaphore(name))

        def sb(ctx, name, shape, dt):
            return ctx.enter_context(nc.sbuf_tensor(name, shape, dt))

        PS = whole.enter_context(nc.psum_tensor("PS", [P, BANKS, 512], F32))

        def bank16(b, dt):
            return PS[:, b, :].bitcast(dt)

        identf = sb(whole, "identf", [P, P], F32)
        identb = sb(whole, "identb", [P, P], BF16)
        d_s = sb(whole, "d_s", [P, NT, 2 * H], F32)
        deg = sb(whole, "deg", [P, NT], F32)
        rdeg = sb(whole, "rdeg", [P, NT], F32)
        a_i = sb(whole, "a_i", [P, H, NT], F32)
        c_i = sb(whole, "c_i", [P, H, NT], F32)
        bias_j = sb(whole, "bias_j", [P, NB, H, NT], F32)

        front = ExitStack()
        XH = sb(front, "XH", [P, NT, F], F32)
        WT = sb(front, "WT", [P, FC, F], F32)
        Wa = sb(front, "Wa", [P, FC, 2 * H], F32)
        rstd = sb(front, "rstd", [P, NT], F32)
        nmr = sb(front, "nmr", [P, NT], F32)

        with ExitStack() as ctx:
            Wl = [sb(ctx, f"Wl{i}", [P, FC, F], F32) for i in range(3)]
            Wc = sb(ctx, "Wc", [P, 2 * FC, F], F32)
            WlT = [WT] + [sb(ctx, f"WlT{i}", [P, FC, F], F32) for i in (1, 2)]
            fused = sb(ctx, "fused", [P, 2 * FC * F + F], F32)
            a_blk = sb(ctx, "a_blk", [P, FC, 2 * H], F32)
            bcol = sb(ctx, "bcol", [P, 2 * FC], F32)
            bwide = sb(ctx, "bwide", [P, 2 * FC, P], F32)
            bc_row = sb(ctx, "bc_row", [P, F], F32)
            stats = sb(ctx, "stats", [P, NT, 6], F32)
            mv = sb(ctx, "mv", [P, NT, 2], F32)
            ve = sb(ctx, "ve", [P, NT], F32)
            sd = sb(ctx, "sd", [P, NT], F32)
            tmp = sb(ctx, "tmp", [P, NT], F32)

            x_in = [sem(f"x_in{i}") for i in range(4)]
            w_in, a_in, b_in, ident_set, a_cleared = (sem(n) for n in ("w_in", "a_in", "b_in", "ident_set", "a_cleared"))
            setup_mm, setup_copied, stats_done, var_ready, sd_ready, dve1, fused_out = (
                sem(n) for n in ("setup_mm", "setup_copied", "stats_done", "var_ready", "sd_ready", "dve1", "fused_out"))

            jobs = []
            for m in range(3):
                for k in range(FC):
                    jobs.append(("T", m, k, WlT[m][:, k, :]))
            for k in range(FC):
                jobs.append(("A", 0, k, Wa[:, k, :]))
            for m in (1, 2):
                for k in range(FC):
                    o = ((m - 1) * FC + k) * F
                    jobs.append(("C", m, k, fused[:, o:o + F]))
            jobs.append(("B", 0, 0, fused[:, 2 * FC * F:]))

            with nc.Block() as block:
                @block.sync
                def _(sp):
                    sp.dma_start(Wl[0][:], W.rearrange("(c p) f -> p c f", p=P)).then_inc(w_in, 16)
                    sp.dma_start(Wl[1][:], W_self.rearrange("(c p) f -> p c f", p=P)).then_inc(w_in, 16)
                    sp.dma_start(Wl[2][:], W_nb.rearrange("(c p) f -> p c f", p=P)).then_inc(w_in, 16)
                    sp.dma_start(Wc[:], W_comb.rearrange("(c p) f -> p c f", p=P)).then_inc(w_in, 16)
                    n = NT // 4
                    for i in range(4):
                        sp.dma_start(XH[:, i * n:(i + 1) * n, :],
                                     x[i * n * P:(i + 1) * n * P, :].rearrange("(t p) f -> p t f", p=P)).then_inc(x_in[i], 16)
                    sp.wait_ge(setup_copied, len(jobs))
                    sp.dma_start(wsc_dram, fused[:]).then_inc(fused_out, 16)
                    sp.wait_ge(fused_out, 16)

                @block.scalar
                def _(act):
                    act.wait_ge(a_cleared, 1)
                    with nc.allow_non_contiguous_dma(reason="64-element columns of the attention vectors"):
                        for h in range(H):
                            rows = slice((h % 2) * D, (h % 2 + 1) * D)
                            for o, a in ((0, a_dst), (H, a_src)):
                                act.dma_start(a_blk[rows, h // 2, o + h:o + h + 1],
                                              a[h, :].rearrange("(d o) -> d o", o=1)).then_inc(a_in, 16)
                        act.dma_start(bcol[:, 0:FC], b_self.rearrange("(c p) -> p c", p=P)).then_inc(b_in, 16)
                        act.dma_start(bcol[:, FC:], b_nb.rearrange("(c p) -> p c", p=P)).then_inc(b_in, 16)
                    act.dma_start(bc_row[:], b_comb.rearrange("(o f) -> o f", o=1).to_broadcast([P, F])).then_inc(b_in, 16)
                    act.wait_ge(var_ready, 1)
                    nc.scalar.activation(sd[:], ve[:], ACT.Sqrt).then_inc(sd_ready, 1)

                @block.gpsimd
                def _(pool):
                    nc.gpsimd.memset(a_blk[:], 0.0).then_inc(a_cleared, 1)
                    nc.gpsimd.memset(identf[:], 0.0).then_inc(ident_set, 1)
                    nc.gpsimd.memset(identb[:], 0.0).then_inc(ident_set, 1)
                    pool.wait_ge(ident_set, 2)
                    for m in (identf, identb):
                        nc.gpsimd.affine_select(out=m[:], in_=m[:], compare_op=ALU.not_equal, fill=1.0, base=0,
                                                pattern=[[-1, P]], channel_multiplier=1).then_inc(ident_set, 1)

                @block.tensor
                def _(pe):
                    pe.wait_ge(ident_set, 4)
                    pe.wait_ge(w_in, 64)
                    for n, (kind, m, k, _) in enumerate(jobs):
                        b = n % BANKS
                        if n >= BANKS:
                            pe.wait_ge(setup_copied, n - BANKS + 1)
                        if kind == "T":
                            for c in range(FC):
                                last = nc.tensor.transpose(PS[:, b, c * P:(c + 1) * P], Wl[m][:, c, k * P:(k + 1) * P], identf[:])
                        elif kind == "A":
                            pe.wait_ge(a_in, 32 * H)
                            for c in range(FC):
                                last = nc.tensor.matmul(PS[:, b, 0:2 * H], Wl[0][:, c, k * P:(k + 1) * P], a_blk[:, c, :],
                                                        start=c == 0, stop=c == FC - 1)
                        elif kind == "C":
                            pe.wait_ge(setup_copied, 3 * FC)
                            for c in range(FC):
                                last = nc.tensor.matmul(PS[:, b, :], WlT[m][:, c, k * P:(k + 1) * P], Wc[:, (m - 1) * FC + c, :],
                                                        start=c == 0, stop=c == FC - 1)
                        else:
                            pe.wait_ge(dve1, 1)
                            for c in range(2 * FC):
                                last = nc.tensor.matmul(PS[:, b, :], bwide[:, c, :], Wc[:, c, :], start=c == 0, stop=c == 2 * FC - 1)
                        last.then_inc(setup_mm, 1)

                @block.vector
                def _(dve):
                    step = [1]

                    def link(ins):
                        step[0] += 1
                        ins.then_inc(dve1, 1)
                        dve.wait_ge(dve1, step[0])

                    dve.wait_ge(b_in, 48)
                    nc.vector.tensor_copy(bwide[:], bcol[:].unsqueeze(2).to_broadcast([P, 2 * FC, P])).then_inc(dve1, 1)
                    for n, (kind, m, k, dst) in enumerate(jobs):
                        dve.wait_ge(setup_mm, n + 1)
                        if kind == "A":
                            nc.vector.tensor_copy(dst, PS[:, n % BANKS, 0:2 * H]).then_inc(setup_copied, 1)
                        elif kind == "B":
                            nc.vector.tensor_tensor(dst, PS[:, n % BANKS, :], bc_row[:], ALU.add).then_inc(setup_copied, 1)
                        else:
                            nc.vector.tensor_copy(dst, PS[:, n % BANKS, :]).then_inc(setup_copied, 1)
                    for t in range(NT):
                        if t % (NT // 4) == 0:
                            dve.wait_ge(x_in[t // (NT // 4)], 16)
                        nc.vector.bn_stats(stats[:, t, :], XH[:, t, :]).then_inc(stats_done, 1)
                    for t in range(NT):
                        dve.wait_ge(stats_done, t + 1)
                        nc.vector.bn_aggr(mv[:, t, :], stats[:, t, :]).then_inc(stats_done, 1)
                    dve.wait_ge(stats_done, 2 * NT)
                    nc.vector.tensor_scalar(ve[:], mv[:, :, 1], EPS, None, ALU.add).then_inc(var_ready, 1)
                    dve.wait_ge(sd_ready, 1)
                    link(nc.vector.reciprocal(rstd[:], sd[:]))
                    link(nc.vector.tensor_tensor(tmp[:], rstd[:], rstd[:], ALU.mult))
                    link(nc.vector.tensor_tensor(tmp[:], tmp[:], ve[:], ALU.mult))
                    link(nc.vector.tensor_scalar(tmp[:], tmp[:], -0.5, 1.5, ALU.mult, ALU.add))
                    link(nc.vector.tensor_tensor(rstd[:], rstd[:], tmp[:], ALU.mult))
                    link(nc.vector.scalar_tensor_tensor(out=nmr[:], in0=mv[:, :, 0], scalar=-1.0, in1=rstd[:],
                                                        op0=ALU.mult, op1=ALU.mult))

        with ExitStack() as ctx:
            adj_in = sb(ctx, "adj_in", [P, 2, TI, JQ], I32)
            mask = sb(ctx, "mask", [P, 2, TI, JQ], BF16)
            stage = sb(ctx, "stage", [P, 2, TQ, IB1], BF16)
            h0 = sb(ctx, "h0", [P, 2, F], F32)
            h0T = sb(ctx, "h0T", [P, 2, FC, P], F32)
            degq = sb(ctx, "degq", [P, NT, 4], F32)
            dg_in = sb(ctx, "dg_in", [P, NT // 2, P], I32)
            dg_bf = sb(ctx, "dg_bf", [P, NT, P], BF16)
            dg_T = sb(ctx, "dg_T", [P, NT, P], BF16)
            dg_0 = dg_bf

            adj_ld = [sem(f"adj_ld{i}") for i in range(2)]
            stage_out = [sem(f"stage_out{i}") for i in range(2)]
            mask_ready, trans_done, stage_ready, h0_ready, h0T_ps, h0T_ready, h_ps, h_copied, ds_copied, deg_done = (
                sem(n) for n in ("mask_ready", "trans_done", "stage_ready", "h0_ready", "h0T_ps", "h0T_ready", "h_ps",
                                 "h_copied", "ds_copied", "deg_done"))
            dg_ld, dg_cast, dg_ps, dg_copied, dg_out = (sem(n) for n in ("dg_ld", "dg_cast", "dg_ps", "dg_copied", "dg_out"))
            B_H0T, B_H, B_DS = 4, 5, 6

            def row(a, n):
                return a[:, bass.ds(n, 1), :].rearrange("p o f -> p (o f)")

            def diagonal(a, first, tiles):
                return bass.AP(tensor=a.tensor, offset=first * (P * N + P), ap=[[N, P], [P * N + P, tiles], [1, P]])

            with nc.Block() as block:
                @block.sync
                def _(sp):
                    for half in range(2):
                        sp.wait_ge(dg_cast, half)
                        sp.dma_start(dg_in[:], diagonal(adj, half * (NT // 2), NT // 2)).then_inc(dg_ld, 16)
                    with sp.Fori(0, NB1) as b:
                        for q in range(4):
                            sp.wait_ge(mask_ready, b * 4 + q + 1)
                            sp.dma_start(adj_in[:, q % 2],
                                         adj[bass.ds(b * IB1, IB1), q * JQ:(q + 1) * JQ].rearrange("(t p) c -> p t c", p=P)
                                         ).then_inc(adj_ld[q % 2], 16)

                @block.gpsimd
                def _(pool):
                    for i in range(2):
                        pool.wait_ge(stage_out[i], 16 * 2 * NB1 + 16)
                    pool.wait_ge(dg_copied, 2)
                    pool.dma_start(diagonal(maskT, 0, NT), dg_0[:]).then_inc(dg_out, 16)
                    pool.dma_start(diag_raw, dg_T[:]).then_inc(dg_out, 16)
                    pool.wait_ge(dg_out, 32)

                @block.vector
                def _(dve):
                    dve.sem_inc(mask_ready, 2)
                    dve.sem_inc(h_copied, 1)
                    dve.sem_inc(ds_copied, 1)
                    for half in range(2):
                        dve.wait_ge(dg_ld, 16 * (half + 1))
                        o = half * (NT // 2)
                        nc.vector.tensor_scalar(dg_bf[:, o:o + NT // 2, :], dg_in[:], 0.0, None, ALU.is_gt).then_inc(dg_cast, 1)
                    dve.wait_ge(dg_ps, 1)
                    v = PS[:, 0:NT // 8, :].bitcast(BF16).rearrange("p b (t c) -> p (b t) c", c=P)
                    nc.vector.tensor_copy(dg_T[:], v).then_inc(dg_copied, 1)
                    dve.wait_ge(dg_copied, 1)
                    nc.vector.tensor_tensor(dg_0[:], dg_T[:], identb[:].unsqueeze(1).to_broadcast([P, NT, P]),
                                            ALU.max).then_inc(dg_copied, 1)
                    with dve.Fori(0, NB1) as b:
                        for q in range(4):
                            n = b * 4 + q
                            dve.wait_ge(adj_ld[q % 2], (b * 2 + q // 2 + 1) * 16)
                            dve.wait_ge(trans_done, (n + 1) * CB)
                            nc.vector.tensor_scalar(mask[:, q % 2], adj_in[:, q % 2], 0.0, None, ALU.is_gt).then_inc(mask_ready, 1)
                            dve.wait_ge(mask_ready, n + 3)
                            nc.vector.tensor_reduce(degq[:, bass.ds(b * TI, TI), q:q + 1].rearrange("p t o -> p (t o)"),
                                                    mask[:, q % 2], AX.X, ALU.add).then_inc(deg_done, 1)
                            dve.wait_ge(h_ps, n + 1)
                            nc.vector.tensor_scalar(row(XH, n), PS[:, B_H, :], 1.0, None, ALU.mult).then_inc(h_copied, 1)
                            nc.vector.tensor_copy(row(d_s, n), PS[:, B_DS, 0:2 * H]).then_inc(ds_copied, 1)
                    dve.wait_ge(deg_done, 4 * NB1)
                    nc.vector.tensor_reduce(deg[:], degq[:], AX.X, ALU.add).then_inc(deg_done, 1)
                    dve.wait_ge(deg_done, 4 * NB1 + 1)
                    nc.vector.tensor_scalar(deg[:], deg[:], 1.0, None, ALU.max).then_inc(deg_done, 1)
                    dve.wait_ge(deg_done, 4 * NB1 + 2)
                    nc.vector.reciprocal(rdeg[:], deg[:]).then_inc(deg_done, 1)

                @block.scalar
                def _(act):
                    act.sem_inc(stage_ready, CB)
                    act.sem_inc(h0T_ready, 1)
                    for i in range(2):
                        act.sem_inc(stage_out[i], 16)
                    with act.Fori(0, NB1) as b:
                        for q in range(4):
                            n = b * 4 + q
                            act.wait_ge(h0T_ps, n + 1)
                            nc.scalar.activation(h0[:, q % 2], row(XH, n), ACT.Relu,
                                                 bias=nmr[:, bass.ds(n, 1)], scale=rstd[:, bass.ds(n, 1)]).then_inc(h0_ready, 1)
                            act.wait_ge(stage_out[q % 2], (b * 2 + q // 2 + 1) * 16)
                            for c in range(CB):
                                act.wait_ge(trans_done, (n + 2) * CB + c + 1)
                                nc.scalar.activation(stage[:, q % 2, 2 * c:2 * c + 2, :],
                                                     bank16(c, BF16).rearrange("p (t i) -> p t i", t=2), ACT.Copy).then_inc(stage_ready, 1)
                            act.wait_ge(h0T_ps, n + 3)
                            nc.scalar.activation(h0T[:, q % 2], PS[:, B_H0T, :].rearrange("p (k c) -> p k c", k=FC),
                                                 ACT.Copy).then_inc(h0T_ready, 1)
                            act.wait_ge(stage_ready, (n + 2) * CB)
                            act.dma_start(maskT[q * JQ:(q + 1) * JQ, bass.ds(b * IB1, IB1)].rearrange("(t p) c -> p t c", p=P),
                                          stage[:, q % 2]).then_inc(stage_out[q % 2], 16)

                @block.tensor
                def _(pe):
                    pe.sem_inc(trans_done, 2 * CB)
                    pe.sem_inc(h0T_ps, 2)
                    pe.wait_ge(dg_cast, 2)
                    for t in range(NT):
                        last = nc.tensor.transpose(bank16(t // 8, BF16)[:, (t % 8) * P:(t % 8 + 1) * P], dg_bf[:, t, :], identb[:])
                    last.then_inc(dg_ps, 1)
                    pe.wait_ge(dg_copied, 1)
                    with pe.Fori(0, NB1) as b:
                        for q in range(4):
                            n = b * 4 + q
                            pe.wait_ge(mask_ready, n + 3)
                            for c in range(CB):
                                pe.wait_ge(stage_ready, n * CB + c + 1)
                                for k in range(2):
                                    for ti in range(TI):
                                        o = (k * TI + ti) * P
                                        last = nc.tensor.transpose(bank16(c, BF16)[:, o:o + P],
                                                                   mask[:, q % 2, ti, (2 * c + k) * P:(2 * c + k + 1) * P], identb[:])
                                last.then_inc(trans_done, 1)
                            pe.wait_ge(h0_ready, n + 1)
                            pe.wait_ge(h0T_ready, n + 1)
                            for k in range(FC):
                                last = nc.tensor.transpose(PS[:, B_H0T, k * P:(k + 1) * P], h0[:, q % 2, k * P:(k + 1) * P], identf[:])
                            last.then_inc(h0T_ps, 1)
                            pe.wait_ge(h_copied, n + 1)
                            pe.wait_ge(ds_copied, n + 1)
                            pe.wait_ge(h0T_ready, n + 2)
                            for k in range(FC):
                                nc.tensor.matmul(PS[:, B_H, :], h0T[:, q % 2, k, :], WT[:, k, :], start=k == 0, stop=k == FC - 1)
                            for k in range(FC):
                                last = nc.tensor.matmul(PS[:, B_DS, 0:2 * H], h0T[:, q % 2, k, :], Wa[:, k, :],
                                                        start=k == 0, stop=k == FC - 1)
                            last.then_inc(h_ps, 1)

        with ExitStack() as ctx:
            bp = sb(ctx, "bp", [P, H, NT], F32)
            bm = sb(ctx, "bm", [P, H, NT], F32)
            dc = sb(ctx, "dc", [P, H, NT], F32)
            t_i = sb(ctx, "t_i", [P, H, NT], F32)
            lk = sb(ctx, "lk", [P, H, NT], F32)
            dmax = sb(ctx, "dmax", [P, H], F32)
            dall = sb(ctx, "dall", [P, H], F32)
            s_T = sb(ctx, "s_T", [NT, H, P], F32)
            val = sb(ctx, "val", [P, 4, NT, DE], F32)
            parts = sb(ctx, "parts", [P, 2, NT, 2, PARTS, DE], BF16)
            dmax_ready, dall_ready, small, exp_done, sT_ps, sT_ready, s_out, val_ready, hi_ready, rest_ready, mid_ready, lo_ready = (
                sem(n) for n in ("dmax_ready", "dall_ready", "small", "exp_done", "sT_ps", "sT_ready", "s_out", "val_ready",
                                 "hi_ready", "rest_ready", "mid_ready", "lo_ready"))
            parts_out = [sem(f"parts_out{i}") for i in range(2)]
            d_v = d_s[:, :, 0:H].rearrange("p t h -> p h t")
            s_v = d_s[:, :, H:2 * H].rearrange("p t h -> p h t")
            dall_b = dall[:].unsqueeze(2).to_broadcast([P, H, NT])

            with nc.Block() as block:
                @block.sync
                def _(sp):
                    sp.wait_ge(sT_ready, 1)
                    for b in range(NB):
                        sp.dma_start(s_rows[b].rearrange("h (k p) -> k h p", p=P), s_T[b * KB:(b + 1) * KB]).then_inc(s_out, 16)
                    for e in range(2):
                        sp.sem_inc(parts_out[e], 16)
                    with sp.Fori(0, H // 2) as hp:
                        for e in range(2):
                            sp.wait_ge(lo_ready, 4 + hp * 4 + 2 * e + 2)
                            sp.dma_start(vals[bass.ds(hp * 2 + e, 1)].rearrange("o p t c -> (o p) (t c)"),
                                         parts[:, e].rearrange("p t s k c -> p (t s k c)")).then_inc(parts_out[e], 16)
                    for e in range(2):
                        sp.wait_ge(parts_out[e], 16 + 16 * (H // 2))
                    sp.wait_ge(s_out, 16 * NB)

                @block.gpsimd
                def _(pool):
                    pool.wait_ge(dmax_ready, 1)
                    nc.gpsimd.partition_all_reduce(dall[:], dmax[:], P, RMAX).then_inc(dall_ready, 1)
                    pool.sem_inc(lo_ready, 4)
                    with pool.Fori(0, H // 2) as hp:
                        for u in range(4):
                            e, s = u // 2, u % 2
                            pool.wait_ge(mid_ready, hp * 4 + u + 1)
                            nc.gpsimd.tensor_tensor(parts[:, e, :, s, 2, :], val[:, u], parts[:, e, :, s, 1, :],
                                                    ALU.subtract).then_inc(lo_ready, 1)

                @block.tensor
                def _(pe):
                    for h in range(H):
                        last = nc.tensor.transpose(PS[0:NT, h // 4, (h % 4) * P:(h % 4 + 1) * P], d_s[:, :, H + h], identf[:])
                    last.then_inc(sT_ps, 1)

                @block.vector
                def _(dve):
                    step = [0]

                    def link(ins):
                        step[0] += 1
                        ins.then_inc(small, 1)
                        dve.wait_ge(small, step[0])

                    nc.vector.tensor_reduce(dmax[:], d_v, AX.X, ALU.max).then_inc(dmax_ready, 1)
                    for b in range(NB):
                        nc.vector.tensor_scalar(bias_j[:, b], d_v, BIG, None, ALU.mult)
                    dve.wait_ge(sT_ps, 1)
                    nc.vector.tensor_scalar(s_T[:], PS[0:NT, 0:2, :].rearrange("t b (h p) -> t (b h) p", p=P), BIG, None,
                                            ALU.mult).then_inc(sT_ready, 1)
                    dve.wait_ge(dall_ready, 1)
                    link(nc.vector.tensor_tensor(dc[:], d_v, dall_b, ALU.subtract))
                    link(nc.vector.tensor_tensor(t_i[:], s_v, dall_b, ALU.add))
                    link(nc.vector.scalar_tensor_tensor(out=lk[:], in0=t_i[:], scalar=SLOPE, in1=t_i[:], op0=ALU.mult, op1=ALU.max))
                    link(nc.vector.tensor_tensor(a_i[:], t_i[:], lk[:], ALU.subtract))
                    link(nc.vector.scalar_tensor_tensor(out=c_i[:], in0=t_i[:], scalar=SLOPE, in1=lk[:], op0=ALU.mult,
                                                        op1=ALU.subtract))
                    dve.wait_ge(exp_done, 2)
                    with dve.Fori(0, H // 2) as hp:
                        def value(u):
                            e, s = u // 2, u % 2
                            b_ = (bp, bm)[s][:, bass.ds(hp * 2 + e, 1), :].rearrange("p o t -> p (o t)")
                            dve.wait_ge(lo_ready, 4 + hp * 4)
                            nc.vector.tensor_tensor(val[:, u, :, 0:D], XH[:, :, bass.ds((hp * 2 + e) * D, D)],
                                                    b_.unsqueeze(2).to_broadcast([P, NT, D]), ALU.mult)
                            nc.vector.tensor_copy(val[:, u, :, D:DE], b_.unsqueeze(2)).then_inc(val_ready, 1)

                        def rest(u):
                            e, s = u // 2, u % 2
                            dve.wait_ge(hi_ready, hp * 4 + u + 1)
                            nc.vector.tensor_tensor(val[:, u], val[:, u], parts[:, e, :, s, 0, :], ALU.subtract).then_inc(rest_ready, 1)

                        value(0)
                        value(1)
                        rest(0)
                        value(2)
                        rest(1)
                        value(3)
                        rest(2)
                        rest(3)

                @block.scalar
                def _(act):
                    act.wait_ge(small, 1)
                    nc.scalar.activation(bp[:], dc[:], ACT.Exp).then_inc(exp_done, 1)
                    nc.scalar.activation(bm[:], dc[:], ACT.Exp, scale=SLOPE).then_inc(exp_done, 1)
                    act.wait_ge(small, 5)
                    nc.scalar.activation(a_i[:], a_i[:], ACT.Exp).then_inc(exp_done, 1)
                    nc.scalar.activation(c_i[:], c_i[:], ACT.Exp).then_inc(exp_done, 1)
                    with act.Fori(0, H // 2) as hp:
                        def hi(u):
                            e, s = u // 2, u % 2
                            if s == 0:
                                act.wait_ge(parts_out[e], 16 + hp * 16)
                            act.wait_ge(val_ready, hp * 4 + u + 1)
                            nc.scalar.activation(parts[:, e, :, s, 0, :], val[:, u], ACT.Copy).then_inc(hi_ready, 1)

                        def mid(u):
                            e, s = u // 2, u % 2
                            act.wait_ge(rest_ready, hp * 4 + u + 1)
                            nc.scalar.activation(parts[:, e, :, s, 1, :], val[:, u], ACT.Copy).then_inc(mid_ready, 1)

                        hi(0)
                        hi(1)
                        mid(0)
                        hi(2)
                        mid(1)
                        hi(3)
                        mid(2)
                        mid(3)
        front.close()

        R = NB * H
        with ExitStack() as ctx:
            mt = sb(ctx, "mt", [P, NT, IB], BF16)
            vt = sb(ctx, "vt", [P, NT, 2 * VW], BF16)
            srow = sb(ctx, "srow", [P, 2, IB], F32)
            stp = sb(ctx, "stp", [P, 2, G, IB], BF16)
            mp = sb(ctx, "mp", [P, 2, G, IB], BF16)
            mm = sb(ctx, "mm", [P, 2, G, IB], BF16)
            acc = sb(ctx, "acc", [P, KB, 2, PARTS, DE], F32)
            zero = sb(ctx, "zero", [P, P], BF16)
            whole_s = sb(ctx, "whole_s", [P, KB, 2, DE], F32)
            joined = sb(ctx, "joined", [P, KB, DE], F32)
            rden = sb(ctx, "rden", [P, KB], F32)
            minus1 = sb(ctx, "minus1", [P, KB], F32)
            o_sb = sb(ctx, "o_sb", [P, KB, D], F32)

            mt_ld = [sem(f"mt_ld{i}") for i in range(2)]
            vt_ld = [sem(f"vt_ld{i}") for i in range(2)]
            srow_ld, srow_used, step_ready, mp_ready, mm_ready, bank_done, acc_ready, acc_free, join, o_out, set_up = (
                sem(n) for n in ("srow_ld", "srow_used", "step_ready", "mp_ready", "mm_ready", "bank_done",
                                 "acc_ready", "acc_free", "join", "o_out", "set_up"))
            ROUND = NG * KB
            JOIN = 7
            bias_f = bias_j[:].rearrange("p b h t -> p (b h t)")

            with nc.Block() as block:
                @block.sync
                def _(sp):
                    def load_srow(b, h):
                        r = b * H + h
                        sp.wait_ge(srow_ld, (r + 1) * 16)
                        sp.wait_ge(srow_used, r + 1)
                        sp.dma_start(srow[:, bass.ds(r % 2, 1)].rearrange("p o i -> p (o i)"),
                                     s_rows[bass.ds(b, 1), bass.ds(h, 1)].rearrange("o q i -> (o q) i").to_broadcast([P, IB])
                                     ).then_inc(srow_ld, 16)

                    def load_groups(b, h, with_mask):
                        r = b * H + h
                        for g in range(NG):
                            js = slice(g * G, (g + 1) * G)
                            sp.wait_ge(bank_done, r * ROUND + (g + 1) * KB)
                            sp.wait_ge(vt_ld[g % 2], (r * (NG // 2) + g // 2 + 1) * 16)
                            sp.dma_start(vt[:, js, :], vals[bass.ds(h, 1), :, js, :].rearrange("o p t c -> (o p) t c")
                                         ).then_inc(vt_ld[g % 2], 16)
                            if with_mask:
                                sp.wait_ge(mt_ld[g % 2], (b * (NG // 2) + g // 2 + 1) * 16)
                                sp.dma_start(mt[:, js, :], maskT[g * G * P:(g + 1) * G * P, bass.ds(b * IB, IB)]
                                             .rearrange("(t p) i -> p t i", p=P)).then_inc(mt_ld[g % 2], 16)

                    for ld in (srow_ld, *vt_ld, *mt_ld):
                        sp.sem_inc(ld, 16)
                    with sp.Fori(0, NB) as b:
                        load_srow(b, 0)
                        load_groups(b, 0, True)
                        with sp.Fori(1, H) as h:
                            load_srow(b, h)
                            load_groups(b, h, False)

                @block.scalar
                def _(act):
                    act.sem_inc(srow_used, 2)
                    act.sem_inc(acc_ready, KB)

                    def steps(r, gp):
                        for e in range(2):
                            act.wait_ge(mp_ready, r * NG + gp * 2 + e + 1)
                            for j in range(G):
                                last = nc.scalar.activation(stp[:, e, j, :], srow[:, bass.ds(r % 2, 1)].rearrange("p o i -> p (o i)"),
                                                            ACT.Relu, bias=bias_f[:, bass.ds(r * NT + gp * (2 * G) + e * G + j, 1)])
                            last.then_inc(step_ready, 1)

                    def copy_out(r):
                        act.wait_ge(acc_free, r + 1)
                        for k in range(KB):
                            act.wait_ge(bank_done, (r + 2) * ROUND - KB + k + 1)
                            nc.scalar.activation(acc[:, k].rearrange("p s q c -> p (s q c)"), PS[:, k, 0:2 * VW],
                                                 ACT.Copy).then_inc(acc_ready, 1)

                    def store(r):
                        act.wait_ge(join, (r + 1) * JOIN)
                        act.dma_start(attn.rearrange("b h p c -> (b h) p c")[bass.ds(r, 1)].rearrange("o p c -> (o p) c"),
                                      o_sb[:].rearrange("p k c -> p (k c)")).then_inc(o_out, 16)

                    act.sem_inc(o_out, 16)
                    act.wait_ge(srow_ld, 32)
                    steps(0, 0)
                    with act.Fori(1, NG // 2) as gp:
                        steps(0, gp)
                    with act.Fori(1, R) as r:
                        act.wait_ge(srow_ld, (r + 2) * 16)
                        steps(r, 0)
                        act.wait_ge(step_ready, r * NG)
                        act.sem_inc(srow_used, 1)
                        copy_out(r - 1)
                        with act.Fori(1, NG // 2) as gp:
                            steps(r, gp)
                        store(r - 1)
                    copy_out(R - 1)
                    store(R - 1)
                    act.wait_ge(o_out, (R + 1) * 16)

                @block.vector
                def _(dve):
                    dve.sem_inc(mp_ready, 2)
                    with dve.Fori(0, NB) as b:
                        with dve.Fori(0, H) as h:
                            with dve.Fori(0, NG // 2) as gp:
                                for e in range(2):
                                    n = (b * H + h) * NG + gp * 2 + e
                                    m_ = mt[:, bass.ds(gp * (2 * G) + e * G, G), :]
                                    dve.wait_ge(step_ready, n + 1)
                                    dve.wait_ge(mt_ld[e], (b * (NG // 2) + gp + 2) * 16)
                                    dve.wait_ge(bank_done, ROUND - KB + n * KB)
                                    nc.vector.tensor_tensor(mp[:, e], stp[:, e], m_, ALU.min).then_inc(mp_ready, 1)
                                    dve.wait_ge(mp_ready, n + 3)
                                    nc.vector.tensor_tensor(mm[:, e], m_, mp[:, e], ALU.subtract).then_inc(mm_ready, 1)

                @block.tensor
                def _(pe):
                    pe.sem_inc(bank_done, ROUND)
                    pe.wait_ge(set_up, 2)
                    with pe.Fori(0, R) as r:
                        pe.wait_ge(acc_ready, (r + 1) * KB)
                        for k in range(KB):
                            nc.tensor.matmul(PS[:, k, 2 * VW:2 * VW + 2], zero[:], zero[:, 0:2], start=True, stop=False,
                                             skip_group_check=True)
                        with pe.Fori(0, NG // 2) as gp:
                            for e in range(2):
                                pe.wait_ge(vt_ld[e], (r * (NG // 2) + gp + 2) * 16)
                                pe.wait_ge(mm_ready, r * NG + gp * 2 + e + 1)
                                for k in range(KB):
                                    for j in range(G):
                                        v = vt[:, bass.ds(gp * (2 * G) + e * G + j, 1), :].rearrange("p o c -> p (o c)")
                                        for s, m_ in ((0, mp), (1, mm)):
                                            last = nc.tensor.matmul(PS[:, k, s * VW:(s + 1) * VW], m_[:, e, j, k * P:(k + 1) * P],
                                                                    v[:, s * VW:(s + 1) * VW], start=False, stop=True,
                                                                    skip_group_check=True)
                                    last.then_inc(bank_done, 1)

                @block.gpsimd
                def _(pool):
                    nc.gpsimd.memset(zero[:], 0.0).then_inc(set_up, 1)
                    nc.gpsimd.memset(minus1[:], -1.0).then_inc(set_up, 1)
                    pool.wait_ge(set_up, 2)
                    pool.sem_inc(acc_free, 1)
                    ks = lambda t_: t_.rearrange("p k s c -> p (k s) c")
                    with pool.Fori(0, NB) as b:
                        with pool.Fori(0, H) as h:
                            r = b * H + h

                            def step(n, ins, *also):
                                ins.then_inc(join, 1)
                                pool.wait_ge(join, r * JOIN + n)

                            def rows_of(c):
                                return c[:, bass.ds(h, 1), bass.ds(b * KB, KB)].rearrange("p o k -> p (o k)").unsqueeze(2) \
                                    .to_broadcast([P, KB, DE])

                            pool.wait_ge(acc_ready, (r + 2) * KB)
                            step(1, nc.gpsimd.tensor_tensor(ks(whole_s), acc[:, :, :, 0, :].rearrange("p k s c -> p (k s) c"),
                                                            acc[:, :, :, 1, :].rearrange("p k s c -> p (k s) c"), ALU.add))
                            step(2, nc.gpsimd.tensor_tensor(ks(whole_s), ks(whole_s),
                                                            acc[:, :, :, 2, :].rearrange("p k s c -> p (k s) c"), ALU.add))
                            pool.sem_inc(acc_free, 1)
                            step(3, nc.gpsimd.tensor_tensor(whole_s[:, :, 0, :], whole_s[:, :, 0, :], rows_of(a_i), ALU.mult))
                            step(4, nc.gpsimd.tensor_tensor(whole_s[:, :, 1, :], whole_s[:, :, 1, :], rows_of(c_i), ALU.mult))
                            step(5, nc.gpsimd.tensor_tensor(joined[:], whole_s[:, :, 0, :], whole_s[:, :, 1, :], ALU.add))
                            step(6, nc.gpsimd.tensor_tensor(rden[:], joined[:, :, D], minus1[:], ALU.pow))
                            pool.wait_ge(o_out, (r + 1) * 16)
                            step(7, nc.gpsimd.tensor_tensor(o_sb[:], joined[:, :, 0:D], rden[:].unsqueeze(2).to_broadcast([P, KB, D]),
                                                            ALU.mult))

        layer1 = ExitStack()
        hh = sb(layer1, "hh", [P, NT, F], FP16)
        hl = sb(layer1, "hl", [P, NT, F], FP16)
        w1 = sb(layer1, "w1", [P, 2 * FC * F + F], F32)
        wsc = w1[:, 0:FC * F].rearrange("p (k f) -> p k f", k=FC)
        wnc = w1[:, FC * F:2 * FC * F].rearrange("p (k f) -> p k f", k=FC)
        bias_row = w1[:, 2 * FC * F:]
        with ExitStack() as ctx:
            x1 = sb(ctx, "x1", [P, 2, KB, F], F32)
            at = sb(ctx, "at", [P, 2, H, KB, D], F32)
            h1 = sb(ctx, "h1", [P, 2, F], F32)
            h1T = sb(ctx, "h1T", [P, 2, FC, P], F32)
            sf = sb(ctx, "sf", [P, 2, F], F32)
            stats1 = sb(ctx, "stats1", [P, KB, 6], F32)
            mv1 = sb(ctx, "mv1", [P, KB, 2], F32)
            ve1, sd1, tmp1 = (sb(ctx, n, [P, KB], F32) for n in ("ve1", "sd1", "tmp1"))
            gate = sb(ctx, "gate", [P, 1], F32)
            rstd1 = sb(ctx, "rstd1", [P, 2, KB], F32)
            nmr1 = sb(ctx, "nmr1", [P, 2, KB], F32)

            in_ld = [sem(f"in_ld{i}") for i in range(2)]
            w1_ld, x1_ready, st1, var1, sd1_ready, ln_ready, h1_ready, hi1, lo1, hT_ps, hT_ready, self_ps, self_ready = (
                sem(n) for n in ("w1_ld", "x1_ready", "st1", "var1", "sd1_ready", "ln_ready", "h1_ready", "hi1", "lo1",
                                 "hT_ps", "hT_ready", "self_ps", "self_ready"))
            x1_out = [sem(f"x1_out{i}") for i in range(2)]
            sf_out = [sem(f"sf_out{i}") for i in range(2)]
            LN = 7

            with nc.Block() as block:
                @block.sync
                def _(sp):
                    sp.dma_start(w1[:], wsc_dram).then_inc(w1_ld, 16)
                    for e in range(2):
                        sp.sem_inc(x1_out[e], 16)
                        sp.sem_inc(sf_out[e], 16)
                    def load(b, e):
                        sp.dma_start(x1[:, e], x[bass.ds(b * IB, IB), :].rearrange("(k p) f -> p k f", p=P)).then_inc(in_ld[e], 16)
                        sp.dma_start(at[:, e].rearrange("p h k d -> p h (k d)"),
                                     attn[bass.ds(b, 1)].rearrange("o h p c -> (o p) h c")).then_inc(in_ld[e], 16)

                    def store(b, bp, e):
                        sp.wait_ge(x1_ready, (b + 1) * KB)
                        sp.dma_start(x1_self[bass.ds(b * KB, KB), :, 0, :].rearrange("k p f -> p k f"), x1[:, e]).then_inc(x1_out[e], 16)
                        for k in range(KB):
                            sp.wait_ge(self_ready, 2 + b * KB + k + 1)
                            sp.dma_start(x1_self[bass.ds(b * KB + k, 1), :, 1, :].rearrange("o p f -> (o p) f"),
                                         sf[:, k % 2]).then_inc(sf_out[k % 2], 16)
                        sp.wait_ge(x1_out[e], (bp + 2) * 16)

                    for e in range(2):
                        load(e, e)
                    with sp.Fori(0, NB // 2 - 1) as bp:
                        for e in range(2):
                            store(bp * 2 + e, bp, e)
                            load(bp * 2 + e + 2, e)
                    for e in range(2):
                        store(NB - 2 + e, NB // 2 - 1, e)
                    for e in range(2):
                        sp.wait_ge(sf_out[e], 16 * NT // 2 + 16)

                @block.gpsimd
                def _(pool):
                    pool.sem_inc(lo1, 2)
                    with pool.Fori(0, NB // 2) as bp:
                        for e in range(2):
                            b = bp * 2 + e
                            for k in range(KB):
                                t = b * KB + k
                                pool.wait_ge(hi1, t + 1)
                                nc.gpsimd.tensor_tensor(hl[:, bass.ds(t, 1)].rearrange("p o f -> p (o f)"), h1[:, k % 2],
                                                        hh[:, bass.ds(t, 1)].rearrange("p o f -> p (o f)"), ALU.subtract).then_inc(lo1, 1)

                @block.vector
                def _(dve):
                    def evacuate(t, k):
                        dve.wait_ge(self_ps, t + 3)
                        dve.wait_ge(sf_out[k % 2], (b * (KB // 2) + k // 2 + 1) * 16)
                        nc.vector.tensor_tensor(sf[:, k % 2], PS[:, 2 + k % 2, :], bias_row, ALU.add).then_inc(self_ready, 1)

                    dve.sem_inc(self_ready, 2)
                    dve.wait_ge(w1_ld, 16)
                    with dve.Fori(0, NB // 2) as bp:
                        for e in range(2):
                            b = bp * 2 + e
                            dve.wait_ge(in_ld[e], (bp + 1) * 32)
                            for k in range(KB):
                                nc.vector.tensor_tensor(x1[:, e, k].rearrange("p (h d) -> p h d", d=D),
                                                        x1[:, e, k].rearrange("p (h d) -> p h d", d=D),
                                                        at[:, e, :, k, :], ALU.add).then_inc(x1_ready, 1)
                            for k in range(KB):
                                dve.wait_ge(x1_ready, b * KB + k + 1)
                                nc.vector.bn_stats(stats1[:, k], x1[:, e, k]).then_inc(st1, 1)
                            dve.wait_ge(st1, b * 2 * KB + KB)
                            nc.vector.memset(gate[:], 0.0)
                            for k in range(KB):
                                nc.vector.bn_aggr(mv1[:, k], stats1[:, k]).then_inc(st1, 1)
                            dve.wait_ge(st1, (b + 1) * 2 * KB)

                            def ln(n, ins):
                                ins.then_inc(ln_ready, 1)
                                dve.wait_ge(ln_ready, b * LN + n)

                            ln(1, nc.vector.tensor_scalar(ve1[:], mv1[:, :, 1], EPS, None, ALU.add))
                            dve.wait_ge(sd1_ready, b + 1)
                            ln(2, nc.vector.reciprocal(rstd1[:, e], sd1[:]))
                            ln(3, nc.vector.tensor_tensor(tmp1[:], rstd1[:, e], rstd1[:, e], ALU.mult))
                            ln(4, nc.vector.tensor_tensor(tmp1[:], tmp1[:], ve1[:], ALU.mult))
                            ln(5, nc.vector.tensor_scalar(tmp1[:], tmp1[:], -0.5, 1.5, ALU.mult, ALU.add))
                            ln(6, nc.vector.tensor_tensor(rstd1[:, e], rstd1[:, e], tmp1[:], ALU.mult))
                            ln(7, nc.vector.scalar_tensor_tensor(out=nmr1[:, e], in0=mv1[:, :, 0], scalar=-1.0, in1=rstd1[:, e],
                                                                 op0=ALU.mult, op1=ALU.mult))
                            for k in range(KB):
                                evacuate(b * KB + k, k)

                @block.scalar
                def _(act):
                    act.sem_inc(hT_ready, 2)
                    with act.Fori(0, NB // 2) as bp:
                        for e in range(2):
                            b = bp * 2 + e
                            act.wait_ge(ln_ready, b * LN + 1)
                            nc.scalar.activation(sd1[:], ve1[:], ACT.Sqrt).then_inc(sd1_ready, 1)
                            act.wait_ge(ln_ready, (b + 1) * LN)
                            for k in range(KB):
                                t = b * KB + k
                                act.wait_ge(lo1, t + 1)
                                act.wait_ge(hT_ps, t + 1)
                                nc.scalar.activation(h1[:, k % 2], x1[:, e, k], ACT.Relu, bias=nmr1[:, e, k:k + 1],
                                                     scale=rstd1[:, e, k:k + 1]).then_inc(h1_ready, 1)
                                act.wait_ge(h1_ready, t + 1)
                                nc.scalar.activation(hh[:, bass.ds(t, 1)].rearrange("p o f -> p (o f)"), h1[:, k % 2], ACT.Copy).then_inc(hi1, 1)
                                act.wait_ge(hT_ps, t + 3)
                                act.wait_ge(self_ps, t + 1)
                                nc.scalar.activation(h1T[:, k % 2], PS[:, k % 2, :].rearrange("p (k c) -> p k c", k=FC), ACT.Copy).then_inc(hT_ready, 1)

                @block.tensor
                def _(pe):
                    pe.sem_inc(hT_ps, 2)
                    pe.sem_inc(self_ps, 2)
                    pe.wait_ge(w1_ld, 16)
                    with pe.Fori(0, NB) as b:
                        def transposes(k):
                            t = b * KB + k
                            pe.wait_ge(h1_ready, t + 1)
                            pe.wait_ge(hT_ready, t + 1)
                            for c in range(FC):
                                last = nc.tensor.transpose(PS[:, k % 2, c * P:(c + 1) * P], h1[:, k % 2, c * P:(c + 1) * P], identf[:])
                            last.then_inc(hT_ps, 1)

                        def product(k):
                            t = b * KB + k
                            pe.wait_ge(hT_ready, t + 3)
                            pe.wait_ge(self_ready, t + 1)
                            for c in range(FC):
                                last = nc.tensor.matmul(PS[:, 2 + k % 2, :], h1T[:, k % 2, c, :], wsc[:, c, :], start=c == 0, stop=c == FC - 1)
                            last.then_inc(self_ps, 1)

                        transposes(0)
                        for k in range(1, KB):
                            transposes(k)
                            product(k - 1)
                        product(KB - 1)

        with ExitStack() as ctx:
            m1 = sb(ctx, "m1", [P, 2, NT, IB1], BF16)
            aggT = sb(ctx, "aggT", [P, FC, IB1], F32)
            xs = sb(ctx, "xs", [P, 2, 2, F], F32)
            y = sb(ctx, "y", [P, F], F32)
            fin = sb(ctx, "fin", [P, 2, F], F32)
            m1_ld = [sem(f"m1_ld{i}") for i in range(2)]
            m1_dg = [sem(f"m1_dg{i}") for i in range(2)]
            xs_ld = [sem(f"xs_ld{i}") for i in range(2)]
            fin_out = [sem(f"fin_out{i}") for i in range(2)]
            agg_ps, aggT_ready, nb_ps, y_ready, fin_ready = (sem(n) for n in ("agg_ps", "aggT_ready", "nb_ps", "y_ready", "fin_ready"))
            JL = 4

            with nc.Block() as block:
                @block.sync
                def _(sp):
                    with sp.Fori(0, NB1 // 2) as bp:
                        for e in range(2):
                            b = bp * 2 + e
                            sp.wait_ge(nb_ps, (b + 1) * TI)
                            sp.dma_start(m1[:, e], maskT[:, bass.ds(b * IB1, IB1)].rearrange("(t p) i -> p t i", p=P)).then_inc(m1_ld[e], 16)
                            sp.wait_ge(m1_ld[e], (bp + 1) * 16)
                            for ti in range(TI):
                                sp.dma_start(m1[:, e, bass.ds(b * TI + ti, 1), ti * P:(ti + 1) * P],
                                             diag_raw[:, bass.ds(b * TI + ti, 1), :]).then_inc(m1_dg[e], 16)

                @block.gpsimd
                def _(pool):
                    with pool.Fori(0, NB1) as b:
                        for ti in range(TI):
                            pool.wait_ge(fin_ready, b * TI + ti + 1)
                            pool.dma_start(xs[:, ti % 2].rearrange("p s f -> p (s f)"),
                                           x1_self[bass.ds(b * TI + ti, 1)].rearrange("o p s f -> (o p) (s f)")).then_inc(xs_ld[ti % 2], 16)

                @block.tensor
                def _(pe):
                    pe.sem_inc(nb_ps, 2 * TI)
                    with pe.Fori(0, NB1 // 2) as bp:
                        for e in range(2):
                            b = bp * 2 + e
                            pe.wait_ge(m1_dg[e], (bp + 1) * 16 * TI)
                            for f in range(FC):
                                pe.wait_ge(aggT_ready, b * FC + f + 1)

                                def tiles(j0, first, last_):
                                    for j in range(JL):
                                        for h_ in (hh, hl):
                                            ins = nc.tensor.matmul(
                                                PS[:, f, :], h_[:, bass.ds(j0 + j, 1), f * P:(f + 1) * P].rearrange("p o c -> p (o c)"),
                                                m1[:, e, bass.ds(j0 + j, 1), :].rearrange("p o c -> p (o c)"),
                                                start=first and j == 0 and h_ is hh, stop=last_ and j == JL - 1 and h_ is hl)
                                    return ins

                                tiles(0, True, False)
                                with pe.Fori(JL, NT - JL, JL) as j0:
                                    tiles(j0, False, False)
                                tiles(NT - JL, False, True).then_inc(agg_ps, 1)
                            pe.wait_ge(aggT_ready, (b + 2) * FC)
                            for ti in range(TI):
                                pe.wait_ge(y_ready, b * TI + ti + 1)
                                for c in range(FC):
                                    last = nc.tensor.matmul(PS[:, 4 + ti % 2, :], aggT[:, c, ti * P:(ti + 1) * P], wnc[:, c, :],
                                                            start=c == 0, stop=c == FC - 1)
                                last.then_inc(nb_ps, 1)

                @block.vector
                def _(dve):
                    dve.sem_inc(fin_ready, 2)
                    dve.sem_inc(y_ready, 2)
                    with dve.Fori(0, NB1) as b:
                        for ti in range(TI):
                            t = b * TI + ti
                            dve.wait_ge(nb_ps, 2 * TI + t + 1)
                            dve.wait_ge(xs_ld[ti % 2], (b * (TI // 2) + ti // 2 + 1) * 16)
                            dve.wait_ge(fin_ready, t + 2)
                            nc.vector.scalar_tensor_tensor(out=y[:], in0=PS[:, 4 + ti % 2, :], scalar=rdeg[:, bass.ds(t, 1)],
                                                           in1=xs[:, ti % 2, 1, :], op0=ALU.mult, op1=ALU.add).then_inc(y_ready, 1)
                            dve.wait_ge(y_ready, t + 3)
                            dve.wait_ge(fin_out[ti % 2], (b * (TI // 2) + ti // 2 + 1) * 16)
                            nc.vector.scalar_tensor_tensor(out=fin[:, ti % 2], in0=y[:], scalar=0.0, in1=xs[:, ti % 2, 0, :],
                                                           op0=ALU.max, op1=ALU.add).then_inc(fin_ready, 1)

                @block.scalar
                def _(act):
                    act.sem_inc(aggT_ready, FC)
                    for e in range(2):
                        act.sem_inc(fin_out[e], 16)
                    with act.Fori(0, NB1) as b:
                        for f in range(FC):
                            act.wait_ge(agg_ps, b * FC + f + 1)
                            act.wait_ge(nb_ps, (b + 2) * TI)
                            nc.scalar.activation(aggT[:, f], PS[:, f, :], ACT.Copy).then_inc(aggT_ready, 1)
                        for ti in range(TI):
                            t = b * TI + ti
                            act.wait_ge(fin_ready, t + 3)
                            act.dma_start(out[bass.ds(t * P, P), :], fin[:, ti % 2]).then_inc(fin_out[ti % 2], 16)
                    for e in range(2):
                        act.wait_ge(fin_out[e], NT // 2 * 16 + 16)
        layer1.close()


_INS = ["x", "adj", "L0_gnn_W", "L0_gnn_a_src", "L0_gnn_a_dst", "L1_gnn_W_self", "L1_gnn_b_self",
        "L1_gnn_W_nb", "L1_gnn_b_nb", "L1_gnn_W_comb", "L1_gnn_b_comb"]


def kernel(**inputs):
    import numpy as _np
    import concourse.bacc as _bacc
    from concourse import mybir as _mybir
    from concourse.bass_utils import run_bass_kernel_spmd as _run

    nc = _bacc.Bacc("TRN2", target_bir_lowering=False, num_devices=1)
    arrays, args = {}, []
    for name in _INS:
        a = _np.ascontiguousarray(inputs[name])
        arrays[f"in_{name}_dram"] = a
        args.append(nc.dram_tensor(f"in_{name}_dram", a.shape, _mybir.dt.from_np(a.dtype), kind="ExternalInput").ap())
    out = nc.dram_tensor("out_0_dram", inputs["x"].shape, _mybir.dt.float32, kind="ExternalOutput").ap()
    build(nc, *args, out)
    r = _run(nc, [arrays], core_ids=[0])
    return r.results[0]["out_0_dram"]
```

```python
import concourse.bass as bass
from concourse import mybir
from contextlib import ExitStack

F32 = mybir.dt.float32
BF16 = mybir.dt.bfloat16
FP16 = mybir.dt.float16
I32 = mybir.dt.int32
ALU = mybir.AluOpType
ACT = mybir.ActivationFunctionType
AX = mybir.AxisListType
RMAX = bass.bass_isa.ReduceOp.max

P = 128
F = 512
FC = F // P
H = 8
D = F // H
DE = D + 1
PP, PM = 3, 2
VP, VALW = PP * DE, (PP + PM) * DE
GSCALE = 2.0 ** 4
MSCALE = 2.0 ** 8
SLOPE = 0.2
EPS = 1e-5
BIG = float(2 ** 60)
IB = 1024
KB = IB // P
IB1 = 512
G = 2
LG = 4
RS, RM = 8, 4
BANKS = 8


def build(nc, x, adj, W, a_src, a_dst, W_self, b_self, W_nb, b_nb, W_comb, b_comb, out):
    N = x.shape[0]
    NT = N // P
    NB = N // IB
    NB1 = N // IB1
    NG = NT // G
    NL = NT // LG
    JQ = N // 4
    TQ = JQ // P
    TI = IB1 // P
    CB = TQ * TI * P // 1024

    def dram(name, shape, dt):
        return nc.dram_tensor(name, shape, dt, kind="Internal").ap()

    maskT = dram("maskT_dram", (N, N), BF16)
    diag_raw = dram("diag_dram", (P, NT, P), BF16)
    s_rows = dram("s_rows_dram", (NB, H, IB), F32)
    vals = dram("vals_dram", (H, P, NT, VALW), BF16)
    attn = dram("attn_dram", (NB, H, P, KB * D), F32)
    x1_self = dram("x1_self_dram", (NT, P, 2, F), F32)
    w1_dram = dram("w1_dram", (P, 2 * FC * F + F), F32)

    whole = ExitStack()
    with whole:
        def sem(name):
            return whole.enter_context(nc.semaphore(name))

        def sb(ctx, name, shape, dt):
            return ctx.enter_context(nc.sbuf_tensor(name, shape, dt))

        PS = whole.enter_context(nc.psum_tensor("PS", [P, BANKS, 512], F32))

        def bank16(b, dt):
            return PS[:, b, :].bitcast(dt)

        identf = sb(whole, "identf", [P, P], F32)
        identb = sb(whole, "identb", [P, P], BF16)
        d_s = sb(whole, "d_s", [P, NT, 2 * H], F32)
        deg = sb(whole, "deg", [P, NT], F32)
        rdeg = sb(whole, "rdeg", [P, NT], F32)
        a_i = sb(whole, "a_i", [P, H, NT], F32)
        c_i = sb(whole, "c_i", [P, H, NT], F32)
        bias_j = sb(whole, "bias_j", [P, NB, H, NT], F32)

        front = ExitStack()
        XH = sb(front, "XH", [P, NT, F], F32)
        with ExitStack() as ctx:
            Wl = sb(ctx, "Wl", [P, FC, F], F32)
            WT = sb(ctx, "WT", [P, FC, F], F32)
            Wa = sb(ctx, "Wa", [P, FC, 2 * H], F32)
            a_blk = sb(ctx, "a_blk", [P, FC, 2 * H], F32)
            rstd = sb(ctx, "rstd", [P, NT], F32)
            nmr = sb(ctx, "nmr", [P, NT], F32)
            stats = sb(ctx, "stats", [P, NT, 6], F32)
            mv = sb(ctx, "mv", [P, NT, 2], F32)
            ve, sd, tmp = (sb(ctx, n, [P, NT], F32) for n in ("ve", "sd", "tmp"))
            adj_in = sb(ctx, "adj_in", [P, 2, TI, JQ], I32)
            mask = sb(ctx, "mask", [P, 2, TI, JQ], BF16)
            stage = sb(ctx, "stage", [P, 2, TQ, IB1], BF16)
            half1, half2, half3 = (sb(ctx, f"half{i}", [P, TI, JQ >> i], BF16) for i in (1, 2, 3))
            h0 = sb(ctx, "h0", [P, 2, F], F32)
            h0T = sb(ctx, "h0T", [P, 2, FC, P], F32)
            degq = sb(ctx, "degq", [P, NT, 4], F32)
            dg_in = sb(ctx, "dg_in", [P, NT // 2, P], I32)
            dg_bf = sb(ctx, "dg_bf", [P, NT, P], BF16)
            dg_T = sb(ctx, "dg_T", [P, NT, P], BF16)
            dg_0 = dg_bf

            XP = 4
            x_in = [sem(f"x_in{i}") for i in range(XP)]
            w_in, a_in, ident_set, a_cleared, w_ps, w_copied, stats_done, var_ready, sd_ready, norm_ready = (
                sem(n) for n in ("w_in", "a_in", "ident_set", "a_cleared", "w_ps", "w_copied", "stats_done", "var_ready",
                                 "sd_ready", "norm_ready"))
            adj_ld = [sem(f"adj_ld{i}") for i in range(2)]
            stage_out = [sem(f"stage_out{i}") for i in range(2)]
            mask_ready, trans_done, stage_ready, h0_ready, h0T_ps, h0T_ready, h_ps, h_copied, ds_copied, halved, deg_done = (
                sem(n) for n in ("mask_ready", "trans_done", "stage_ready", "h0_ready", "h0T_ps", "h0T_ready", "h_ps",
                                 "h_copied", "ds_copied", "halved", "deg_done"))
            dg_ld, dg_cast, dg_ps, dg_copied, dg_out = (sem(n) for n in ("dg_ld", "dg_cast", "dg_ps", "dg_copied", "dg_out"))
            B_H0T, B_H, B_DS = 4, 5, 6

            def row(a, n):
                return a[:, bass.ds(n, 1), :].rearrange("p o f -> p (o f)")

            def diagonal(a, first, tiles):
                return bass.AP(tensor=a.tensor, offset=first * (P * N + P), ap=[[N, P], [P * N + P, tiles], [1, P]])

            with nc.Block() as block:
                @block.sync
                def _(sp):
                    sp.dma_start(Wl[:], W.rearrange("(c p) f -> p c f", p=P)).then_inc(w_in, 16)
                    n = NT // XP
                    for i in range(XP):
                        sp.dma_start(XH[:, i * n:(i + 1) * n, :],
                                     x[i * n * P:(i + 1) * n * P, :].rearrange("(t p) f -> p t f", p=P)).then_inc(x_in[i], 16)
                    for half in range(2):
                        sp.wait_ge(dg_cast, half)
                        sp.dma_start(dg_in[:], diagonal(adj, half * (NT // 2), NT // 2)).then_inc(dg_ld, 16)
                    with sp.Fori(0, NB1) as b:
                        for q in range(4):
                            sp.wait_ge(mask_ready, b * 4 + q + 1)
                            sp.dma_start(adj_in[:, q % 2],
                                         adj[bass.ds(b * IB1, IB1), q * JQ:(q + 1) * JQ].rearrange("(t p) c -> p t c", p=P)
                                         ).then_inc(adj_ld[q % 2], 16)

                @block.gpsimd
                def _(pool):
                    nc.gpsimd.memset(a_blk[:], 0.0).then_inc(a_cleared, 1)
                    nc.gpsimd.memset(identf[:], 0.0).then_inc(ident_set, 1)
                    nc.gpsimd.memset(identb[:], 0.0).then_inc(ident_set, 1)
                    pool.wait_ge(ident_set, 2)
                    for m in (identf, identb):
                        nc.gpsimd.affine_select(out=m[:], in_=m[:], compare_op=ALU.not_equal, fill=1.0, base=0,
                                                pattern=[[-1, P]], channel_multiplier=1).then_inc(ident_set, 1)
                    pool.wait_ge(dg_copied, 2)
                    pool.dma_start(diag_raw, dg_T[:]).then_inc(dg_out, 16)
                    for i in range(2):
                        pool.wait_ge(stage_out[i], 16 * 2 * NB1 + 16)
                    pool.dma_start(diagonal(maskT, 0, NT), dg_0[:]).then_inc(dg_out, 16)
                    pool.wait_ge(dg_out, 32)

                @block.vector
                def _(dve):
                    dve.wait_ge(w_ps, 1)
                    nc.vector.tensor_copy(WT[:], PS[:, 0:FC, :]).then_inc(w_copied, 1)
                    dve.wait_ge(w_ps, 2)
                    nc.vector.tensor_copy(Wa[:], PS[:, FC, 0:FC * 2 * H].rearrange("p (k h) -> p k h", k=FC)).then_inc(w_copied, 1)
                    for t in range(NT):
                        if t % (NT // XP) == 0:
                            dve.wait_ge(x_in[t // (NT // XP)], 16)
                        nc.vector.bn_stats(stats[:, t, :], XH[:, t, :]).then_inc(stats_done, 1)
                    for t in range(NT):
                        dve.wait_ge(stats_done, t + 1)
                        nc.vector.bn_aggr(mv[:, t, :], stats[:, t, :]).then_inc(stats_done, 1)
                    dve.wait_ge(stats_done, 2 * NT)
                    nc.vector.tensor_scalar(ve[:], mv[:, :, 1], EPS, None, ALU.add).then_inc(var_ready, 1)

                    step = [0]

                    def link(ins):
                        step[0] += 1
                        ins.then_inc(norm_ready, 1)
                        dve.wait_ge(norm_ready, step[0])

                    dve.wait_ge(sd_ready, 1)
                    link(nc.vector.reciprocal(rstd[:], sd[:]))
                    link(nc.vector.tensor_tensor(tmp[:], rstd[:], rstd[:], ALU.mult))
                    link(nc.vector.tensor_tensor(tmp[:], tmp[:], ve[:], ALU.mult))
                    link(nc.vector.tensor_scalar(tmp[:], tmp[:], -0.5, 1.5, ALU.mult, ALU.add))
                    link(nc.vector.tensor_tensor(rstd[:], rstd[:], tmp[:], ALU.mult))
                    link(nc.vector.scalar_tensor_tensor(out=nmr[:], in0=mv[:, :, 0], scalar=-1.0, in1=rstd[:],
                                                        op0=ALU.mult, op1=ALU.mult))
                    dve.sem_inc(mask_ready, 2)
                    for half in range(2):
                        dve.wait_ge(dg_ld, 16 * (half + 1))
                        o = half * (NT // 2)
                        nc.vector.tensor_scalar(dg_bf[:, o:o + NT // 2, :], dg_in[:], 0.0, None, ALU.is_gt).then_inc(dg_cast, 1)
                    dve.wait_ge(dg_ps, 1)
                    v = PS[:, 0:NT // 8, :].bitcast(BF16).rearrange("p b (t c) -> p (b t) c", c=P)
                    nc.vector.tensor_copy(dg_T[:], v).then_inc(dg_copied, 1)
                    dve.wait_ge(dg_copied, 1)
                    nc.vector.tensor_tensor(dg_0[:], dg_T[:], identb[:].unsqueeze(1).to_broadcast([P, NT, P]),
                                            ALU.max).then_inc(dg_copied, 1)
                    dve.sem_inc(h_copied, 1)
                    dve.sem_inc(ds_copied, 1)

                    def cast(b, q, e):
                        dve.wait_ge(adj_ld[q % 2], (e + q // 2 + 1) * 16)
                        dve.wait_ge(trans_done, (b * 4 + q + 1) * CB)
                        nc.vector.tensor_scalar(mask[:, q % 2], adj_in[:, q % 2], 0.0, None, ALU.is_gt).then_inc(mask_ready, 1)

                    def degrees(b, q):
                        n = b * 4 + q
                        dve.wait_ge(mask_ready, n + 3)
                        src = mask[:, q % 2]
                        for i, dst in enumerate((half1, half2, half3)):
                            w = JQ >> (i + 1)
                            nc.vector.tensor_tensor(dst[:], src[:, :, 0:w], src[:, :, w:2 * w], ALU.add).then_inc(halved, 1)
                            dve.wait_ge(halved, n * 3 + i + 1)
                            src = dst
                        nc.vector.tensor_reduce(degq[:, bass.ds(b * TI, TI), q:q + 1].rearrange("p t o -> p (t o)"),
                                                half3[:], AX.X, ALU.add).then_inc(deg_done, 1)

                    def products_out(b, q):
                        n = b * 4 + q
                        dve.wait_ge(h_ps, n + 1)
                        nc.vector.tensor_scalar(row(XH, n), PS[:, B_H, :], 1.0, None, ALU.mult).then_inc(h_copied, 1)
                        nc.vector.tensor_copy(row(d_s, n), PS[:, B_DS, 0:2 * H]).then_inc(ds_copied, 1)

                    def quarters(b, last):
                        for q in range(4):
                            if q < 3:
                                cast(b, q + 1, b * 2)
                            elif not last:
                                cast(b + 1, 0, b * 2 + 2)
                            degrees(b, q)
                            products_out(b, q)

                    cast(0, 0, 0)
                    with dve.Fori(0, NB1 - 1) as b:
                        quarters(b, False)
                    quarters(NB1 - 1, True)
                    dve.wait_ge(deg_done, 4 * NB1)
                    nc.vector.tensor_reduce(deg[:], degq[:], AX.X, ALU.add).then_inc(deg_done, 1)
                    dve.wait_ge(deg_done, 4 * NB1 + 1)
                    nc.vector.tensor_scalar(deg[:], deg[:], 1.0, GSCALE, ALU.max, ALU.mult).then_inc(deg_done, 1)
                    dve.wait_ge(deg_done, 4 * NB1 + 2)
                    nc.vector.reciprocal(rdeg[:], deg[:]).then_inc(deg_done, 1)

                @block.scalar
                def _(act):
                    act.wait_ge(a_cleared, 1)
                    with nc.allow_non_contiguous_dma(reason="64-element columns of the attention vectors"):
                        for h in range(H):
                            rows = slice((h % 2) * D, (h % 2 + 1) * D)
                            for o, a in ((0, a_dst), (H, a_src)):
                                act.dma_start(a_blk[rows, h // 2, o + h:o + h + 1],
                                              a[h, :].rearrange("(d o) -> d o", o=1)).then_inc(a_in, 16)
                    act.wait_ge(var_ready, 1)
                    nc.scalar.activation(sd[:], ve[:], ACT.Sqrt).then_inc(sd_ready, 1)
                    act.wait_ge(norm_ready, 6)
                    act.sem_inc(stage_ready, CB)
                    act.sem_inc(h0T_ready, 1)
                    for i in range(2):
                        act.sem_inc(stage_out[i], 16)
                    with act.Fori(0, NB1) as b:
                        for q in range(4):
                            n = b * 4 + q
                            act.wait_ge(h0T_ps, n + 1)
                            nc.scalar.activation(h0[:, q % 2], row(XH, n), ACT.Relu,
                                                 bias=nmr[:, bass.ds(n, 1)], scale=rstd[:, bass.ds(n, 1)]).then_inc(h0_ready, 1)
                            act.wait_ge(h0T_ps, n + 3)
                            nc.scalar.activation(h0T[:, q % 2], PS[:, B_H0T, :].rearrange("p (k c) -> p k c", k=FC),
                                                 ACT.Copy).then_inc(h0T_ready, 1)
                            act.wait_ge(stage_out[q % 2], (b * 2 + q // 2 + 1) * 16)
                            for c in range(CB):
                                act.wait_ge(trans_done, (n + 2) * CB + c + 1)
                                nc.scalar.activation(stage[:, q % 2, 2 * c:2 * c + 2, :],
                                                     bank16(c, BF16).rearrange("p (t i) -> p t i", t=2), ACT.Copy).then_inc(stage_ready, 1)
                            act.wait_ge(stage_ready, (n + 2) * CB)
                            act.dma_start(maskT[q * JQ:(q + 1) * JQ, bass.ds(b * IB1, IB1)].rearrange("(t p) c -> p t c", p=P),
                                          stage[:, q % 2]).then_inc(stage_out[q % 2], 16)

                @block.tensor
                def _(pe):
                    pe.wait_ge(ident_set, 4)
                    pe.wait_ge(w_in, 16)
                    for k in range(FC):
                        for c in range(FC):
                            last = nc.tensor.transpose(PS[:, k, c * P:(c + 1) * P], Wl[:, c, k * P:(k + 1) * P], identf[:])
                    last.then_inc(w_ps, 1)
                    pe.wait_ge(a_in, 32 * H)
                    for k in range(FC):
                        for c in range(FC):
                            last = nc.tensor.matmul(PS[:, FC, k * 2 * H:(k + 1) * 2 * H], Wl[:, c, k * P:(k + 1) * P], a_blk[:, c, :],
                                                    start=c == 0, stop=c == FC - 1)
                    last.then_inc(w_ps, 1)
                    pe.sem_inc(trans_done, 2 * CB)
                    pe.sem_inc(h0T_ps, 2)
                    pe.wait_ge(w_copied, 2)
                    pe.wait_ge(dg_cast, 2)
                    for t in range(NT):
                        last = nc.tensor.transpose(bank16(t // 8, BF16)[:, (t % 8) * P:(t % 8 + 1) * P], dg_bf[:, t, :], identb[:])
                    last.then_inc(dg_ps, 1)
                    pe.wait_ge(dg_copied, 1)
                    with pe.Fori(0, NB1) as b:
                        for q in range(4):
                            n = b * 4 + q
                            pe.wait_ge(mask_ready, n + 3)
                            for c in range(CB):
                                pe.wait_ge(stage_ready, n * CB + c + 1)
                                for k in range(2):
                                    for ti in range(TI):
                                        o = (k * TI + ti) * P
                                        last = nc.tensor.transpose(bank16(c, BF16)[:, o:o + P],
                                                                   mask[:, q % 2, ti, (2 * c + k) * P:(2 * c + k + 1) * P], identb[:])
                                last.then_inc(trans_done, 1)
                            pe.wait_ge(h0_ready, n + 1)
                            pe.wait_ge(h0T_ready, n + 1)
                            for k in range(FC):
                                last = nc.tensor.transpose(PS[:, B_H0T, k * P:(k + 1) * P], h0[:, q % 2, k * P:(k + 1) * P], identf[:])
                            last.then_inc(h0T_ps, 1)
                            pe.wait_ge(h_copied, n + 1)
                            pe.wait_ge(ds_copied, n + 1)
                            pe.wait_ge(h0T_ready, n + 2)
                            for k in range(FC):
                                nc.tensor.matmul(PS[:, B_H, :], h0T[:, q % 2, k, :], WT[:, k, :], start=k == 0, stop=k == FC - 1)
                            for k in range(FC):
                                last = nc.tensor.matmul(PS[:, B_DS, 0:2 * H], h0T[:, q % 2, k, :], Wa[:, k, :],
                                                        start=k == 0, stop=k == FC - 1)
                            last.then_inc(h_ps, 1)

        with ExitStack() as ctx:
            bp = sb(ctx, "bp", [P, H, NT], F32)
            bm = sb(ctx, "bm", [P, H, NT], F32)
            dc = sb(ctx, "dc", [P, H, NT], F32)
            t_i = sb(ctx, "t_i", [P, H, NT], F32)
            lk = sb(ctx, "lk", [P, H, NT], F32)
            dmax = sb(ctx, "dmax", [P, H], F32)
            dall = sb(ctx, "dall", [P, H], F32)
            s_T = sb(ctx, "s_T", [NT, H, P], F32)
            val = sb(ctx, "val", [P, 2, 2, NT, DE], F32)
            parts = sb(ctx, "parts", [P, 2, NT, VALW], BF16)
            Wp = sb(ctx, "Wp", [P, FC, F], F32)
            WpT = sb(ctx, "WpT", [P, FC, F], F32)
            Wc = sb(ctx, "Wc", [P, FC, F], F32)
            fused = sb(ctx, "fused", [P, 2 * FC + 1, F], F32)
            bcol = sb(ctx, "bcol", [P, 2 * FC], F32)
            bwide = sb(ctx, "bwide", [P, 2 * FC, P], F32)
            bc_row = sb(ctx, "bc_row", [P, F], F32)
            dmax_ready, dall_ready, small, exp_done, sT_ps, sT_ready, s_out = (
                sem(n) for n in ("dmax_ready", "dall_ready", "small", "exp_done", "sT_ps", "sT_ready", "s_out"))
            val_ready, hi_ready, rest_ready, mid_ready, minus_ready, plus_ready = (
                sem(n) for n in ("val_ready", "hi_ready", "rest_ready", "mid_ready", "minus_ready", "plus_ready"))
            parts_out = [sem(f"parts_out{i}") for i in range(2)]
            b_in, wide, fused_ps, fused_copied, fused_out = (sem(n) for n in ("b_in", "wide", "fused_ps", "fused_copied", "fused_out"))
            wp_in = [sem(f"wp_in{i}") for i in range(2)]
            wc_in = [sem(f"wc_in{i}") for i in range(2)]
            B_W, B_BIAS = 2, 7
            d_v = d_s[:, :, 0:H].rearrange("p t h -> p h t")
            s_v = d_s[:, :, H:2 * H].rearrange("p t h -> p h t")
            dall_b = dall[:].unsqueeze(2).to_broadcast([P, H, NT])

            def part(e, i):
                p = parts[:, e, :, i * DE:(i + 1) * DE]
                return p if i < PP else p.bitcast(FP16)

            with nc.Block() as block:
                @block.sync
                def _(sp):
                    for e in range(2):
                        sp.sem_inc(parts_out[e], 16)
                    sp.dma_start(Wp[:], W_self.rearrange("(c p) f -> p c f", p=P)).then_inc(wp_in[0], 16)
                    sp.dma_start(Wc[:], W_comb[0:F, :].rearrange("(c p) f -> p c f", p=P)).then_inc(wc_in[0], 16)
                    sp.wait_ge(sT_ready, 1)
                    for b in range(NB):
                        sp.dma_start(s_rows[b].rearrange("h (k p) -> k h p", p=P), s_T[b * KB:(b + 1) * KB]).then_inc(s_out, 16)
                    sp.wait_ge(fused_ps, 1)
                    sp.dma_start(Wp[:], W_nb.rearrange("(c p) f -> p c f", p=P)).then_inc(wp_in[1], 16)
                    sp.wait_ge(fused_ps, 2)
                    sp.dma_start(Wc[:], W_comb[F:2 * F, :].rearrange("(c p) f -> p c f", p=P)).then_inc(wc_in[1], 16)
                    for h in range(H):
                        sp.wait_ge(minus_ready, h + 1)
                        sp.wait_ge(plus_ready, h + 3)
                        sp.dma_start(vals[h], parts[:, h % 2]).then_inc(parts_out[h % 2], 16)
                    sp.wait_ge(wide, 2)
                    sp.dma_start(w1_dram, fused[:].rearrange("p k f -> p (k f)")).then_inc(fused_out, 16)
                    for e in range(2):
                        sp.wait_ge(parts_out[e], 16 + 16 * (H // 2))
                    sp.wait_ge(s_out, 16 * NB)
                    sp.wait_ge(fused_out, 16)

                @block.gpsimd
                def _(pool):
                    with nc.allow_non_contiguous_dma(reason="bias columns"):
                        pool.dma_start(bcol[:, 0:FC], b_self.rearrange("(c p) -> p c", p=P)).then_inc(b_in, 16)
                        pool.dma_start(bcol[:, FC:], b_nb.rearrange("(c p) -> p c", p=P)).then_inc(b_in, 16)
                    pool.dma_start(bc_row[:], b_comb.rearrange("(o f) -> o f", o=1).to_broadcast([P, F])).then_inc(b_in, 16)
                    pool.wait_ge(dmax_ready, 1)
                    nc.gpsimd.partition_all_reduce(dall[:], dmax[:], P, RMAX).then_inc(dall_ready, 1)
                    pool.wait_ge(b_in, 48)
                    nc.gpsimd.tensor_copy(bwide[:], bcol[:].unsqueeze(2).to_broadcast([P, 2 * FC, P])).then_inc(wide, 1)
                    pool.sem_inc(plus_ready, 2)
                    with pool.Fori(0, H // 2) as hp:
                        for e in range(2):
                            pool.wait_ge(mid_ready, hp * 2 + e + 1)
                            nc.gpsimd.tensor_tensor(part(e, 2), val[:, e, 0], part(e, 1), ALU.subtract).then_inc(plus_ready, 1)

                @block.tensor
                def _(pe):
                    for h in range(H):
                        last = nc.tensor.transpose(PS[0:NT, h // 4, (h % 4) * P:(h % 4 + 1) * P], d_s[:, :, H + h], identf[:])
                    last.then_inc(sT_ps, 1)
                    for i in range(2):
                        pe.wait_ge(wp_in[i], 16)
                        if i:
                            pe.wait_ge(fused_copied, 2)
                        for k in range(FC):
                            for c in range(FC):
                                last = nc.tensor.transpose(PS[:, B_W + k, c * P:(c + 1) * P], Wp[:, c, k * P:(k + 1) * P], identf[:])
                        last.then_inc(fused_ps, 1)
                        pe.wait_ge(wc_in[i], 16)
                        pe.wait_ge(wide, 1)
                        for c in range(FC):
                            nc.tensor.matmul(PS[:, B_BIAS, :], bwide[:, i * FC + c, :], Wc[:, c, :],
                                             start=i == 0 and c == 0, stop=i == 1 and c == FC - 1)
                        pe.wait_ge(fused_copied, 2 * i + 1)
                        for k in range(FC):
                            for c in range(FC):
                                last = nc.tensor.matmul(PS[:, B_W + k, :], WpT[:, c, k * P:(k + 1) * P], Wc[:, c, :],
                                                        start=c == 0, stop=c == FC - 1)
                        last.then_inc(fused_ps, 1)

                @block.vector
                def _(dve):
                    step = [0]

                    def link(ins):
                        step[0] += 1
                        ins.then_inc(small, 1)
                        dve.wait_ge(small, step[0])

                    nc.vector.tensor_reduce(dmax[:], d_v, AX.X, ALU.max).then_inc(dmax_ready, 1)
                    for b in range(NB):
                        nc.vector.tensor_scalar(bias_j[:, b], d_v, BIG, None, ALU.mult)
                    dve.wait_ge(sT_ps, 1)
                    nc.vector.tensor_scalar(s_T[:], PS[0:NT, 0:2, :].rearrange("t b (h p) -> t (b h) p", p=P), BIG, None,
                                            ALU.mult).then_inc(sT_ready, 1)
                    dve.wait_ge(dall_ready, 1)
                    link(nc.vector.tensor_tensor(dc[:], d_v, dall_b, ALU.subtract))
                    link(nc.vector.tensor_tensor(t_i[:], s_v, dall_b, ALU.add))
                    link(nc.vector.scalar_tensor_tensor(out=lk[:], in0=t_i[:], scalar=SLOPE, in1=t_i[:], op0=ALU.mult, op1=ALU.max))
                    link(nc.vector.tensor_tensor(a_i[:], t_i[:], lk[:], ALU.subtract))
                    link(nc.vector.scalar_tensor_tensor(out=c_i[:], in0=t_i[:], scalar=SLOPE, in1=lk[:], op0=ALU.mult,
                                                        op1=ALU.subtract))
                    dve.wait_ge(exp_done, 4)
                    link(nc.vector.tensor_scalar(bm[:], bm[:], MSCALE, None, ALU.mult))
                    link(nc.vector.tensor_scalar(c_i[:], c_i[:], 1.0 / MSCALE, None, ALU.mult))
                    with dve.Fori(0, H // 2) as hp:
                        def value(e, s):
                            b_ = (bp, bm)[s][:, bass.ds(hp * 2 + e, 1), :].rearrange("p o t -> p (o t)")
                            nc.vector.tensor_tensor(val[:, e, s, :, 0:D], XH[:, :, bass.ds((hp * 2 + e) * D, D)],
                                                    b_.unsqueeze(2).to_broadcast([P, NT, D]), ALU.mult)
                            nc.vector.tensor_copy(val[:, e, s, :, D:DE], b_.unsqueeze(2)).then_inc(val_ready, 1)

                        def rest(e):
                            dve.wait_ge(hi_ready, hp * 4 + e * 2 + 1)
                            nc.vector.tensor_tensor(val[:, e, 0], val[:, e, 0], part(e, 0), ALU.subtract).then_inc(rest_ready, 1)

                        def minus_rest(e):
                            dve.wait_ge(hi_ready, hp * 4 + e * 2 + 2)
                            nc.vector.tensor_tensor(part(e, 4), val[:, e, 1], part(e, 3), ALU.subtract).then_inc(minus_ready, 1)

                        dve.wait_ge(plus_ready, hp * 2 + 1)
                        value(0, 0)
                        value(0, 1)
                        rest(0)
                        dve.wait_ge(plus_ready, hp * 2 + 2)
                        value(1, 0)
                        minus_rest(0)
                        value(1, 1)
                        rest(1)
                        minus_rest(1)
                    dve.wait_ge(fused_copied, 5)
                    nc.vector.tensor_tensor(fused[:, 2 * FC, :], fused[:, 2 * FC, :], bc_row[:], ALU.add).then_inc(wide, 1)

                @block.scalar
                def _(act):
                    def copied(dst, b0, banks, done):
                        act.wait_ge(fused_ps, done)
                        nc.scalar.activation(dst, PS[:, b0:b0 + banks, :], ACT.Copy).then_inc(fused_copied, 1)

                    act.wait_ge(small, 1)
                    nc.scalar.activation(bp[:], dc[:], ACT.Exp).then_inc(exp_done, 1)
                    nc.scalar.activation(bm[:], dc[:], ACT.Exp, scale=SLOPE).then_inc(exp_done, 1)
                    act.wait_ge(small, 5)
                    nc.scalar.activation(a_i[:], a_i[:], ACT.Exp).then_inc(exp_done, 1)
                    nc.scalar.activation(c_i[:], c_i[:], ACT.Exp).then_inc(exp_done, 1)
                    for hp in range(H // 2):
                        def hi(e, s):
                            act.wait_ge(val_ready, hp * 4 + e * 2 + s + 1)
                            nc.scalar.activation(part(e, s * PP), val[:, e, s], ACT.Copy).then_inc(hi_ready, 1)

                        def mid(e):
                            act.wait_ge(rest_ready, hp * 2 + e + 1)
                            nc.scalar.activation(part(e, 1), val[:, e, 0], ACT.Copy).then_inc(mid_ready, 1)

                        act.wait_ge(parts_out[0], (hp + 1) * 16)
                        hi(0, 0)
                        hi(0, 1)
                        mid(0)
                        act.wait_ge(parts_out[1], (hp + 1) * 16)
                        hi(1, 0)
                        hi(1, 1)
                        mid(1)
                        i = hp // 2
                        if hp % 2 == 0:
                            copied(WpT[:], B_W, FC, 2 * i + 1)
                        else:
                            copied(fused[:, i * FC:(i + 1) * FC, :], B_W, FC, 2 * i + 2)
                    copied(fused[:, 2 * FC, :].unsqueeze(1), B_BIAS, 1, 4)
        front.close()

        R = NB * H
        with ExitStack() as ctx:
            mt = sb(ctx, "mt", [P, NT, IB], BF16)
            vt = sb(ctx, "vt", [P, NT, VALW], BF16)
            srow = sb(ctx, "srow", [P, 2, IB], F32)
            stp = sb(ctx, "stp", [P, RS, G, IB], BF16)
            mp = sb(ctx, "mp", [P, RM, G, IB], BF16)
            mm = sb(ctx, "mm", [P, RM, G, IB], BF16)
            acc = sb(ctx, "acc", [P, KB, PP + PM, DE], F32)
            whole_s = sb(ctx, "whole_s", [P, KB, 2, DE], F32)
            joined = sb(ctx, "joined", [P, KB, DE], F32)
            rden = sb(ctx, "rden", [P, KB], F32)
            minus1 = sb(ctx, "minus1", [P, KB], F32)
            o_sb = sb(ctx, "o_sb", [P, KB, D], F32)

            mt_ld = [sem(f"mt_ld{i}") for i in range(2)]
            vt_ld = [sem(f"vt_ld{i}") for i in range(2)]
            srow_ld, srow_used, step_ready, mp_ready, mm_ready, bank_done, acc_ready, acc_free, join, o_out, set_up = (
                sem(n) for n in ("srow_ld", "srow_used", "step_ready", "mp_ready", "mm_ready", "bank_done",
                                 "acc_ready", "acc_free", "join", "o_out", "set_up"))
            ROUND = NG * KB
            JOIN = 7
            bias_f = bias_j[:].rearrange("p b h t -> p (b h t)")

            with nc.Block() as block:
                @block.sync
                def _(sp):
                    def load_srow(b, h):
                        r = b * H + h
                        sp.wait_ge(srow_ld, (r + 1) * 16)
                        sp.wait_ge(srow_used, r + 1)
                        sp.dma_start(srow[:, bass.ds(r % 2, 1)].rearrange("p o i -> p (o i)"),
                                     s_rows[bass.ds(b, 1), bass.ds(h, 1)].rearrange("o q i -> (o q) i").to_broadcast([P, IB])
                                     ).then_inc(srow_ld, 16)

                    def load_groups(b, h, with_mask):
                        r = b * H + h
                        for l in range(NL):
                            js = slice(l * LG, (l + 1) * LG)
                            sp.wait_ge(bank_done, r * ROUND + (l + 1) * (LG // G) * KB)
                            sp.wait_ge(vt_ld[l % 2], (r * (NL // 2) + l // 2 + 1) * 16)
                            sp.dma_start(vt[:, js, :], vals[bass.ds(h, 1), :, js, :].rearrange("o p t c -> (o p) t c")
                                         ).then_inc(vt_ld[l % 2], 16)
                            if with_mask:
                                sp.wait_ge(mt_ld[l % 2], (b * (NL // 2) + l // 2 + 1) * 16)
                                sp.dma_start(mt[:, js, :], maskT[l * LG * P:(l + 1) * LG * P, bass.ds(b * IB, IB)]
                                             .rearrange("(t p) i -> p t i", p=P)).then_inc(mt_ld[l % 2], 16)

                    for ld in (srow_ld, *vt_ld, *mt_ld):
                        sp.sem_inc(ld, 16)
                    with sp.Fori(0, NB) as b:
                        load_srow(b, 0)
                        load_groups(b, 0, True)
                        with sp.Fori(1, H) as h:
                            load_srow(b, h)
                            load_groups(b, h, False)

                @block.scalar
                def _(act):
                    act.sem_inc(srow_used, 2)
                    act.sem_inc(acc_ready, KB)

                    def steps(r, c):
                        for u in range(RS):
                            act.wait_ge(mp_ready, r * NG + c * RS + u + 1)
                            for j in range(G):
                                last = nc.scalar.activation(stp[:, u, j, :], srow[:, bass.ds(r % 2, 1)].rearrange("p o i -> p (o i)"),
                                                            ACT.Relu, bias=bias_f[:, bass.ds(r * NT + c * (RS * G) + u * G + j, 1)])
                            last.then_inc(step_ready, 1)

                    def copy_out(r):
                        act.wait_ge(acc_free, r + 1)
                        for k in range(KB):
                            act.wait_ge(bank_done, (r + 2) * ROUND - KB + k + 1)
                            nc.scalar.activation(acc[:, k].rearrange("p q c -> p (q c)"), PS[:, k, 0:VALW],
                                                 ACT.Copy).then_inc(acc_ready, 1)

                    def store(r):
                        act.wait_ge(join, (r + 1) * JOIN)
                        act.dma_start(attn.rearrange("b h p c -> (b h) p c")[bass.ds(r, 1)].rearrange("o p c -> (o p) c"),
                                      o_sb[:].rearrange("p k c -> p (k c)")).then_inc(o_out, 16)

                    act.sem_inc(o_out, 16)
                    act.wait_ge(srow_ld, 32)
                    steps(0, 0)
                    with act.Fori(1, NG // RS) as c:
                        steps(0, c)
                    with act.Fori(1, R) as r:
                        act.wait_ge(srow_ld, (r + 2) * 16)
                        steps(r, 0)
                        act.wait_ge(step_ready, r * NG)
                        act.sem_inc(srow_used, 1)
                        copy_out(r - 1)
                        with act.Fori(1, NG // RS) as c:
                            steps(r, c)
                        store(r - 1)
                    copy_out(R - 1)
                    store(R - 1)
                    act.wait_ge(o_out, (R + 1) * 16)

                @block.vector
                def _(dve):
                    dve.sem_inc(mp_ready, RS)
                    with dve.Fori(0, NB) as b:
                        with dve.Fori(0, H) as h:
                            with dve.Fori(0, NG // RS) as c:
                                def group(u):
                                    return (b * H + h) * NG + c * RS + u, mt[:, bass.ds(c * (RS * G) + u * G, G), :]

                                def plus(u):
                                    n, m_ = group(u)
                                    l = u * G // LG
                                    dve.wait_ge(step_ready, n + 1)
                                    dve.wait_ge(mt_ld[l % 2], (b * (NL // 2) + c * (RS * G // LG // 2) + l // 2 + 2) * 16)
                                    dve.wait_ge(bank_done, ROUND - (RM - 1) * KB + n * KB)
                                    nc.vector.tensor_tensor(mp[:, u % RM], stp[:, u], m_, ALU.min).then_inc(mp_ready, 1)

                                def minus(u):
                                    n, m_ = group(u)
                                    dve.wait_ge(mp_ready, n + RS + 1)
                                    nc.vector.tensor_tensor(mm[:, u % RM], m_, mp[:, u % RM], ALU.subtract).then_inc(mm_ready, 1)

                                for u in range(0, RS, 2):
                                    plus(u)
                                    plus(u + 1)
                                    minus(u)
                                    minus(u + 1)

                @block.tensor
                def _(pe):
                    pe.sem_inc(bank_done, ROUND)

                    def group(r, c, u, opens):
                        l = u * G // LG
                        pe.wait_ge(vt_ld[l % 2], (r * (NL // 2) + c * (RM * G // LG // 2) + l // 2 + 2) * 16)
                        pe.wait_ge(mm_ready, r * NG + c * RM + u + 1)
                        for k in range(KB):
                            if opens:
                                pe.wait_ge(acc_ready, r * KB + k + 1)
                            for j in range(G):
                                v = vt[:, bass.ds(c * (RM * G) + u * G + j, 1), :].rearrange("p o c -> p (o c)")
                                first = opens and j == 0
                                nc.tensor.matmul(PS[:, k, 0:VP], mp[:, u, j, k * P:(k + 1) * P], v[:, 0:VP],
                                                 start=first, stop=not first, skip_group_check=True)
                                last = nc.tensor.matmul(PS[:, k, VP:VALW], mm[:, u, j, k * P:(k + 1) * P], v[:, VP:VALW].bitcast(FP16),
                                                        start=False, stop=True, skip_group_check=True)
                            last.then_inc(bank_done, 1)

                    with pe.Fori(0, R) as r:
                        for u in range(RM):
                            group(r, 0, u, u == 0)
                        with pe.Fori(1, NG // RM) as c:
                            for u in range(RM):
                                group(r, c, u, False)

                @block.gpsimd
                def _(pool):
                    nc.gpsimd.memset(minus1[:], -1.0).then_inc(set_up, 1)
                    pool.wait_ge(set_up, 1)
                    pool.sem_inc(acc_free, 1)
                    with pool.Fori(0, NB) as b:
                        with pool.Fori(0, H) as h:
                            r = b * H + h

                            def step(n, ins, *also):
                                ins.then_inc(join, 1)
                                pool.wait_ge(join, r * JOIN + n)

                            def rows_of(c):
                                return c[:, bass.ds(h, 1), bass.ds(b * KB, KB)].rearrange("p o k -> p (o k)").unsqueeze(2) \
                                    .to_broadcast([P, KB, DE])

                            pool.wait_ge(acc_ready, (r + 2) * KB)
                            step(1, nc.gpsimd.tensor_tensor(whole_s[:], acc[:, :, 0:PP + 1:PP, :], acc[:, :, 1:PP + 2:PP, :], ALU.add))
                            step(2, nc.gpsimd.tensor_tensor(whole_s[:, :, 0, :], whole_s[:, :, 0, :], acc[:, :, 2, :], ALU.add))
                            pool.sem_inc(acc_free, 1)
                            step(3, nc.gpsimd.tensor_tensor(whole_s[:, :, 0, :], whole_s[:, :, 0, :], rows_of(a_i), ALU.mult))
                            step(4, nc.gpsimd.tensor_tensor(whole_s[:, :, 1, :], whole_s[:, :, 1, :], rows_of(c_i), ALU.mult))
                            step(5, nc.gpsimd.tensor_tensor(joined[:], whole_s[:, :, 0, :], whole_s[:, :, 1, :], ALU.add))
                            step(6, nc.gpsimd.tensor_tensor(rden[:], joined[:, :, D], minus1[:], ALU.pow))
                            pool.wait_ge(o_out, (r + 1) * 16)
                            step(7, nc.gpsimd.tensor_tensor(o_sb[:], joined[:, :, 0:D], rden[:].unsqueeze(2).to_broadcast([P, KB, D]),
                                                            ALU.mult))

        layer1 = ExitStack()
        gh = sb(layer1, "gh", [P, NT, F], FP16)
        gl = sb(layer1, "gl", [P, NT, F], FP16)
        m1a = sb(layer1, "m1a", [P, NT, IB1], BF16)
        m1_ld = [whole.enter_context(nc.semaphore(f"m1_ld{i}")) for i in range(2)]
        m1_dg = [whole.enter_context(nc.semaphore(f"m1_dg{i}")) for i in range(2)]

        def load_mask(sp, m1_, e, b, count):
            sp.dma_start(m1_[:], maskT[:, bass.ds(b * IB1, IB1)].rearrange("(t p) i -> p t i", p=P)).then_inc(m1_ld[e], 16)
            sp.wait_ge(m1_ld[e], count * 16)
            for ti in range(TI):
                sp.dma_start(m1_[:, bass.ds(b * TI + ti, 1), ti * P:(ti + 1) * P],
                             diag_raw[:, bass.ds(b * TI + ti, 1), :]).then_inc(m1_dg[e], 16)

        with ExitStack() as ctx:
            x1 = sb(ctx, "x1", [P, 2, KB, F], F32)
            at = sb(ctx, "at", [P, 2, H, KB, D], F32)
            w1 = sb(ctx, "w1", [P, 2 * FC * F + F], F32)
            wsc = w1[:, 0:FC * F].rearrange("p (k f) -> p k f", k=FC)
            wnc = w1[:, FC * F:2 * FC * F].rearrange("p (k f) -> p k f", k=FC)
            bias_row = w1[:, 2 * FC * F:]
            h1 = sb(ctx, "h1", [P, 2, F], F32)
            h1T = sb(ctx, "h1T", [P, 2, FC, P], F32)
            sf = sb(ctx, "sf", [P, 2, F], F32)
            stats1 = sb(ctx, "stats1", [P, KB, 6], F32)
            mv1 = sb(ctx, "mv1", [P, KB, 2], F32)
            ve1, sd1, tmp1 = (sb(ctx, n, [P, KB], F32) for n in ("ve1", "sd1", "tmp1"))
            gate = sb(ctx, "gate", [P, 1], F32)
            rstd1 = sb(ctx, "rstd1", [P, 2, KB], F32)
            nmr1 = sb(ctx, "nmr1", [P, 2, KB], F32)

            in_ld = [sem(f"in_ld{i}") for i in range(2)]
            w1_ld, x1_ready, st1, sd1_ready, ln_ready, h1_ready, hT_ps, hT_ready, both_ps, self_ready, gh_ready, gl_ready = (
                sem(n) for n in ("w1_ld", "x1_ready", "st1", "sd1_ready", "ln_ready", "h1_ready", "hT_ps", "hT_ready",
                                 "both_ps", "self_ready", "gh_ready", "gl_ready"))
            x1_out = [sem(f"x1_out{i}") for i in range(2)]
            sf_out = [sem(f"sf_out{i}") for i in range(2)]
            LN = 7
            PAIR = 2 * KB
            NPAIR = NB // 2

            with nc.Block() as block:
                @block.sync
                def _(sp):
                    def load(b, e):
                        sp.dma_start(x1[:, e], x[bass.ds(b * IB, IB), :].rearrange("(k p) f -> p k f", p=P)).then_inc(in_ld[e], 16)
                        sp.dma_start(at[:, e].rearrange("p h k d -> p h (k d)"),
                                     attn[bass.ds(b, 1)].rearrange("o h p c -> (o p) h c")).then_inc(in_ld[e], 16)

                    def store(b, bp, e):
                        sp.wait_ge(x1_ready, (b + 1) * KB)
                        sp.dma_start(x1_self[bass.ds(b * KB, KB), :, 0, :].rearrange("k p f -> p k f"), x1[:, e]).then_inc(x1_out[e], 16)
                        for k in range(KB):
                            sp.wait_ge(self_ready, 2 + b * KB + k + 1)
                            sp.dma_start(x1_self[bass.ds(b * KB + k, 1), :, 1, :].rearrange("o p f -> (o p) f"),
                                         sf[:, k % 2]).then_inc(sf_out[k % 2], 16)
                        sp.wait_ge(x1_out[e], (bp + 2) * 16)

                    for e in range(2):
                        sp.sem_inc(x1_out[e], 16)
                        sp.sem_inc(sf_out[e], 16)
                    load(0, 0)
                    sp.dma_start(w1[:], w1_dram).then_inc(w1_ld, 16)
                    load(1, 1)
                    load_mask(sp, m1a, 0, 0, 1)
                    with sp.Fori(0, NPAIR - 1) as bp:
                        for e in range(2):
                            store(bp * 2 + e, bp, e)
                            load(bp * 2 + e + 2, e)
                    for e in range(2):
                        store(NB - 2 + e, NPAIR - 1, e)
                    for e in range(2):
                        sp.wait_ge(sf_out[e], 16 * NT // 2 + 16)

                @block.vector
                def _(dve):
                    def residual(b, bp, e, k):
                        if k == 0:
                            dve.wait_ge(in_ld[e], (bp + 1) * 32)
                        nc.vector.tensor_tensor(x1[:, e, k].rearrange("p (h d) -> p h d", d=D),
                                                x1[:, e, k].rearrange("p (h d) -> p h d", d=D),
                                                at[:, e, :, k, :], ALU.add).then_inc(x1_ready, 1)
                        dve.wait_ge(x1_ready, b * KB + k + 1)
                        nc.vector.bn_stats(stats1[:, k], x1[:, e, k]).then_inc(st1, 1)

                    def coefficients(b, e):
                        dve.wait_ge(st1, b * 2 * KB + KB)
                        nc.vector.memset(gate[:], 0.0)
                        for k in range(KB):
                            nc.vector.bn_aggr(mv1[:, k], stats1[:, k]).then_inc(st1, 1)
                        dve.wait_ge(st1, (b + 1) * 2 * KB)

                        def ln(n, ins):
                            ins.then_inc(ln_ready, 1)
                            dve.wait_ge(ln_ready, b * LN + n)

                        ln(1, nc.vector.tensor_scalar(ve1[:], mv1[:, :, 1], EPS, None, ALU.add))
                        dve.wait_ge(sd1_ready, b + 1)
                        ln(2, nc.vector.reciprocal(rstd1[:, e], sd1[:]))
                        ln(3, nc.vector.tensor_tensor(tmp1[:], rstd1[:, e], rstd1[:, e], ALU.mult))
                        ln(4, nc.vector.tensor_tensor(tmp1[:], tmp1[:], ve1[:], ALU.mult))
                        ln(5, nc.vector.tensor_scalar(tmp1[:], tmp1[:], -0.5, 1.5, ALU.mult, ALU.add))
                        ln(6, nc.vector.tensor_tensor(rstd1[:, e], rstd1[:, e], tmp1[:], ALU.mult))
                        ln(7, nc.vector.scalar_tensor_tensor(out=nmr1[:, e], in0=mv1[:, :, 0], scalar=-1.0, in1=rstd1[:, e],
                                                             op0=ALU.mult, op1=ALU.mult))

                    def products_out(b, k):
                        t = b * KB + k
                        dve.wait_ge(both_ps, t + 3)
                        dve.wait_ge(sf_out[k % 2], (b * (KB // 2) + k // 2 + 1) * 16)
                        nc.vector.tensor_tensor(sf[:, k % 2], PS[:, 2 + k % 2, :], bias_row, ALU.add).then_inc(self_ready, 1)
                        dve.wait_ge(gh_ready, t + 1)
                        nc.vector.scalar_tensor_tensor(out=gl[:, bass.ds(t, 1)].rearrange("p o f -> p (o f)"), in0=PS[:, 4 + k % 2, :],
                                                       scalar=GSCALE, in1=gh[:, bass.ds(t, 1)].rearrange("p o f -> p (o f)"),
                                                       op0=ALU.mult, op1=ALU.subtract).then_inc(gl_ready, 1)

                    def tiles(b, bp, e, ahead):
                        for k in range(KB):
                            if ahead and k < KB // 2:
                                residual(b + 1, bp + e, 1 - e, 2 * k)
                                residual(b + 1, bp + e, 1 - e, 2 * k + 1)
                            if ahead and k == KB // 2:
                                coefficients(b + 1, 1 - e)
                            products_out(b, k)

                    dve.sem_inc(self_ready, 2)
                    dve.sem_inc(gl_ready, 2)
                    for k in range(KB):
                        residual(0, 0, 0, k)
                    coefficients(0, 0)
                    dve.wait_ge(w1_ld, 16)
                    with dve.Fori(0, NPAIR - 1) as bp:
                        tiles(bp * 2, bp, 0, True)
                        tiles(bp * 2 + 1, bp, 1, True)
                    tiles(NB - 2, NPAIR - 1, 0, True)
                    tiles(NB - 1, NPAIR - 1, 1, False)

                @block.scalar
                def _(act):
                    def root(b):
                        act.wait_ge(ln_ready, b * LN + 1)
                        nc.scalar.activation(sd1[:], ve1[:], ACT.Sqrt).then_inc(sd1_ready, 1)

                    def normalise(t, p):
                        e, k = p // KB, p % KB
                        act.wait_ge(hT_ps, t + 1)
                        nc.scalar.activation(h1[:, k % 2], x1[:, e, k], ACT.Relu, bias=nmr1[:, e, k:k + 1],
                                             scale=rstd1[:, e, k:k + 1]).then_inc(h1_ready, 1)

                    def transposed(t, p):
                        act.wait_ge(hT_ps, t + 3)
                        act.wait_ge(both_ps, t + 1)
                        nc.scalar.activation(h1T[:, p % 2], PS[:, p % 2, :].rearrange("p (k c) -> p k c", k=FC), ACT.Copy).then_inc(hT_ready, 1)

                    def high(t, p):
                        act.wait_ge(both_ps, t + 3)
                        nc.scalar.activation(gh[:, bass.ds(t, 1)].rearrange("p o f -> p (o f)"), PS[:, 4 + p % 2, :], ACT.Copy,
                                             scale=GSCALE).then_inc(gh_ready, 1)

                    def tiles(bp, last):
                        t0 = bp * PAIR
                        for p in range(PAIR):
                            if p == KB // 2 + 1:
                                root(bp * 2 + 1)
                                act.wait_ge(ln_ready, (bp * 2 + 2) * LN)
                            if p == KB + KB // 2 + 1 and not last:
                                root(bp * 2 + 2)
                                act.wait_ge(ln_ready, (bp * 2 + 3) * LN)
                            if p > 0:
                                high(t0 + p - 1, p - 1)
                            if p < PAIR - 1 or not last:
                                transposed(t0 + p + 1, p + 1)
                            if p < PAIR - 2 or not last:
                                normalise(t0 + p + 2, (p + 2) % PAIR)
                        high(t0 + PAIR - 1, PAIR - 1)

                    root(0)
                    act.wait_ge(ln_ready, LN)
                    act.sem_inc(hT_ready, 2)
                    normalise(0, 0)
                    transposed(0, 0)
                    normalise(1, 1)
                    with act.Fori(0, NPAIR - 1) as bp:
                        tiles(bp, False)
                    tiles(NPAIR - 1, True)

                @block.tensor
                def _(pe):
                    def transposes(t, k):
                        pe.wait_ge(h1_ready, t + 1)
                        pe.wait_ge(hT_ready, t + 1)
                        for c in range(FC):
                            last = nc.tensor.transpose(PS[:, k % 2, c * P:(c + 1) * P], h1[:, k % 2, c * P:(c + 1) * P], identf[:])
                        last.then_inc(hT_ps, 1)

                    def products(t, k):
                        pe.wait_ge(hT_ready, t + 3)
                        pe.wait_ge(self_ready, t + 1)
                        pe.wait_ge(gl_ready, t + 1)
                        for w_, bank in ((wsc, 2), (wnc, 4)):
                            for c in range(FC):
                                last = nc.tensor.matmul(PS[:, bank + k % 2, :], h1T[:, k % 2, c, :], w_[:, c, :], start=c == 0, stop=c == FC - 1)
                        last.then_inc(both_ps, 1)

                    pe.sem_inc(hT_ps, 2)
                    pe.sem_inc(both_ps, 2)
                    pe.wait_ge(w1_ld, 16)
                    transposes(0, 0)
                    with pe.Fori(0, NB - 1) as b:
                        for k in range(KB):
                            transposes(b * KB + k + 1, k + 1)
                            products(b * KB + k, k)
                    for k in range(KB):
                        t = (NB - 1) * KB + k
                        if k < KB - 1:
                            transposes(t + 1, k + 1)
                        products(t, k)

        with ExitStack() as ctx:
            m1b = sb(ctx, "m1b", [P, NT, IB1], BF16)
            xs = sb(ctx, "xs", [P, 4, 2, F], F32)
            y = sb(ctx, "y", [P, F], F32)
            fin = sb(ctx, "fin", [P, 2, F], F32)
            xs_ld = [sem(f"xs_ld{i}") for i in range(TI)]
            fin_out = [sem(f"fin_out{i}") for i in range(2)]
            sum_ps, y_ready, fin_ready = (sem(n) for n in ("sum_ps", "y_ready", "fin_ready"))
            JL = 4

            with nc.Block() as block:
                @block.sync
                def _(sp):
                    load_mask(sp, m1b, 1, 1, 1)
                    with sp.Fori(0, NB1 // 2 - 1) as bp:
                        for e, m1_ in enumerate((m1a, m1b)):
                            sp.wait_ge(sum_ps, (bp * 2 + e + 1) * TI)
                            load_mask(sp, m1_, e, bp * 2 + 2 + e, bp + 2)

                @block.gpsimd
                def _(pool):
                    with pool.Fori(0, NB1) as b:
                        for ti in range(TI):
                            pool.wait_ge(fin_ready, b * TI + ti + 1)
                            pool.dma_start(xs[:, ti].rearrange("p s f -> p (s f)"),
                                           x1_self[bass.ds(b * TI + ti, 1)].rearrange("o p s f -> (o p) (s f)")).then_inc(xs_ld[ti], 16)

                @block.tensor
                def _(pe):
                    with pe.Fori(0, NB1 // 2) as bp:
                        for e, m1_ in enumerate((m1a, m1b)):
                            pe.wait_ge(m1_dg[e], (bp + 1) * 16 * TI)
                            for ti in range(TI):
                                pe.wait_ge(y_ready, (bp * 2 + e) * TI + ti + 1)

                                def tiles(j0, first, last_):
                                    for j in range(JL):
                                        for g_ in (gh, gl):
                                            ins = nc.tensor.matmul(
                                                PS[:, ti, :], m1_[:, bass.ds(j0 + j, 1), ti * P:(ti + 1) * P].rearrange("p o c -> p (o c)"),
                                                g_[:, bass.ds(j0 + j, 1), :].rearrange("p o c -> p (o c)"),
                                                start=first and j == 0 and g_ is gh, stop=last_ and j == JL - 1 and g_ is gl)
                                    return ins

                                tiles(0, True, False)
                                with pe.Fori(JL, NT - JL, JL) as j0:
                                    tiles(j0, False, False)
                                tiles(NT - JL, False, True).then_inc(sum_ps, 1)

                @block.vector
                def _(dve):
                    dve.sem_inc(fin_ready, TI)
                    dve.sem_inc(y_ready, TI)
                    with dve.Fori(0, NB1) as b:
                        for ti in range(TI):
                            t = b * TI + ti
                            dve.wait_ge(xs_ld[ti], (b + 1) * 16)
                            dve.wait_ge(fin_ready, t + TI)
                            dve.wait_ge(sum_ps, t + 1)
                            nc.vector.scalar_tensor_tensor(out=y[:], in0=PS[:, ti, :], scalar=rdeg[:, bass.ds(t, 1)],
                                                           in1=xs[:, ti, 1, :], op0=ALU.mult, op1=ALU.add).then_inc(y_ready, 1)
                            dve.wait_ge(y_ready, t + TI + 1)
                            dve.wait_ge(fin_out[ti % 2], (b * (TI // 2) + ti // 2 + 1) * 16)
                            nc.vector.scalar_tensor_tensor(out=fin[:, ti % 2], in0=y[:], scalar=0.0, in1=xs[:, ti, 0, :],
                                                           op0=ALU.max, op1=ALU.add).then_inc(fin_ready, 1)

                @block.scalar
                def _(act):
                    for e in range(2):
                        act.sem_inc(fin_out[e], 16)
                    with act.Fori(0, NB1) as b:
                        for ti in range(TI):
                            t = b * TI + ti
                            act.wait_ge(fin_ready, t + TI + 1)
                            act.dma_start(out[bass.ds(t * P, P), :], fin[:, ti % 2]).then_inc(fin_out[ti % 2], 16)
                    for e in range(2):
                        act.wait_ge(fin_out[e], NT // 2 * 16 + 16)
        layer1.close()


_INS = ["x", "adj", "L0_gnn_W", "L0_gnn_a_src", "L0_gnn_a_dst", "L1_gnn_W_self", "L1_gnn_b_self",
        "L1_gnn_W_nb", "L1_gnn_b_nb", "L1_gnn_W_comb", "L1_gnn_b_comb"]


def kernel(**inputs):
    import numpy as _np
    import concourse.bacc as _bacc
    from concourse import mybir as _mybir
    from concourse.bass_utils import run_bass_kernel_spmd as _run

    nc = _bacc.Bacc("TRN2", target_bir_lowering=False, num_devices=1)
    arrays, args = {}, []
    for name in _INS:
        a = _np.ascontiguousarray(inputs[name])
        arrays[f"in_{name}_dram"] = a
        args.append(nc.dram_tensor(f"in_{name}_dram", a.shape, _mybir.dt.from_np(a.dtype), kind="ExternalInput").ap())
    out = nc.dram_tensor("out_0_dram", inputs["x"].shape, _mybir.dt.float32, kind="ExternalOutput").ap()
    build(nc, *args, out)
    r = _run(nc, [arrays], core_ids=[0])
    return r.results[0]["out_0_dram"]
```

```python
import concourse.bass as bass
from concourse import mybir
from contextlib import ExitStack

F32 = mybir.dt.float32
BF16 = mybir.dt.bfloat16
FP16 = mybir.dt.float16
I32 = mybir.dt.int32
ALU = mybir.AluOpType
ACT = mybir.ActivationFunctionType
AX = mybir.AxisListType
RMAX = bass.bass_isa.ReduceOp.max

P = 128
F = 512
FC = F // P
H = 8
D = F // H
DE = D + 1
PP, PM = 3, 2
VP, VALW = PP * DE, (PP + PM) * DE
MSCALE = 2.0 ** 8
GSCALE = 2.0 ** 4
HSCALE = 2.0 ** 8
WSCALE = 2.0 ** 6
SLOPE = 0.2
EPS = 1e-5
BIG = float(2 ** 60)
IB = 1024
KB = IB // P
IB1 = 512
G = 2
LG = 4
RS, RM = 8, 4
BANKS = 8


def build(nc, x, adj, W, a_src, a_dst, W_self, b_self, W_nb, b_nb, W_comb, b_comb, out):
    N = x.shape[0]
    NT = N // P
    NB = N // IB
    NB1 = N // IB1
    NG = NT // G
    NL = NT // LG
    JQ = N // 4
    TQ = JQ // P
    TI = IB1 // P
    CB = TQ * TI * P // 1024

    def dram(name, shape, dt):
        return nc.dram_tensor(name, shape, dt, kind="Internal").ap()

    maskT = dram("maskT_dram", (N, N), BF16)
    diag_raw = dram("diag_dram", (P, NT, P), BF16)
    s_rows = dram("s_rows_dram", (NB, H, IB), F32)
    vals = dram("vals_dram", (H, P, NT, VALW), BF16)
    attn = dram("attn_dram", (NB, H, P, KB * D), F32)
    x1_self = dram("x1_self_dram", (NT, P, 2, F), F32)

    whole = ExitStack()
    with whole:
        def sem(name):
            return whole.enter_context(nc.semaphore(name))

        def sb(ctx, name, shape, dt):
            return ctx.enter_context(nc.sbuf_tensor(name, shape, dt))

        PS = whole.enter_context(nc.psum_tensor("PS", [P, BANKS, 512], F32))

        def bank16(b, dt):
            return PS[:, b, :].bitcast(dt)

        identf = sb(whole, "identf", [P, P], F32)
        identb = sb(whole, "identb", [P, P], BF16)
        identh = sb(whole, "identh", [P, P], FP16)
        d_s = sb(whole, "d_s", [P, NT, 2 * H], F32)
        deg = sb(whole, "deg", [P, NT], F32)
        rdeg = sb(whole, "rdeg", [P, NT], F32)
        a_i = sb(whole, "a_i", [P, H, NT], F32)
        c_i = sb(whole, "c_i", [P, H, NT], F32)
        bias_j = sb(whole, "bias_j", [P, NB, H, NT], F32)

        region = sb(whole, "region", [P, NT * F], F32)
        XH = region[:].rearrange("p (t f) -> p t f", t=NT)
        mt = region[:].bitcast(BF16).rearrange("p (t i) -> p t i", t=NT)
        x1 = region[:, 0:2 * KB * F].rearrange("p (e k f) -> p e k f", e=2, k=KB)
        at = region[:, 2 * KB * F:].rearrange("p (e h k d) -> p e h k d", e=2, h=H, k=KB)
        m1b = region[:, 2 * KB * F:].bitcast(BF16).rearrange("p (t i) -> p t i", t=NT)

        fused = sb(whole, "fused", [P, 2 * FC + 1, F], F32)
        w_parts = fused[:, 0:2 * FC, :].bitcast(FP16).rearrange("p k (s f) -> p k s f", s=2)
        bias_row = fused[:, 2 * FC, :]
        dg_bf = dg_0 = fused[:, 0:NT * P // (2 * F), :].bitcast(BF16).rearrange("p k (t c) -> p (k t) c", c=P)
        dg_in0 = fused[:, FC:FC + NT * P // (2 * F), :].bitcast(I32).rearrange("p k (t c) -> p (k t) c", c=P)

        with ExitStack() as ctx:
            Wl = sb(ctx, "Wl", [P, FC, F], F32)
            WT = sb(ctx, "WT", [P, FC, F], F32)
            Wa = sb(ctx, "Wa", [P, FC, 2 * H], F32)
            a_col = sb(ctx, "a_col", [P, 2, FC], F32)
            a_blk = sb(ctx, "a_blk", [P, FC, 2 * H], F32)
            rstd = sb(ctx, "rstd", [P, NT], F32)
            nmr = sb(ctx, "nmr", [P, NT], F32)
            stats = sb(ctx, "stats", [P, NT, 6], F32)
            mv = sb(ctx, "mv", [P, NT, 2], F32)
            ve, sd, tmp = (sb(ctx, n, [P, NT], F32) for n in ("ve", "sd", "tmp"))
            adj_in = sb(ctx, "adj_in", [P, 2, TI, JQ], I32)
            mask = sb(ctx, "mask", [P, 2, TI, JQ], BF16)
            stage = sb(ctx, "stage", [P, 2, TQ, IB1], BF16)
            half1, half2, half3 = (sb(ctx, f"half{i}", [P, TI, JQ >> i], BF16) for i in (1, 2, 3))
            h0 = sb(ctx, "h0", [P, 2, F], F32)
            h0T = sb(ctx, "h0T", [P, 2, FC, P], F32)
            degq = sb(ctx, "degq", [P, NT, 4], F32)
            dg_T = sb(ctx, "dg_T", [P, NT, P], BF16)

            dg_in = (dg_in0, stage[:, 0].bitcast(I32).rearrange("p t (a c) -> p (t a) c", c=P))

            XP = 4
            x_in = [sem(f"x_in{i}") for i in range(XP)]
            w_in, a_in, a_set, ident_set, a_cleared, w_ps, w_copied, stats_done, var_ready, sd_ready, norm_ready = (
                sem(n) for n in ("w_in", "a_in", "a_set", "ident_set", "a_cleared", "w_ps", "w_copied", "stats_done", "var_ready",
                                 "sd_ready", "norm_ready"))
            adj_ld = [sem(f"adj_ld{i}") for i in range(2)]
            stage_out = [sem(f"stage_out{i}") for i in range(2)]
            mask_ready, trans_done, stage_ready, h0_ready, h0T_ps, h0T_ready, h_ps, h_copied, ds_copied, halved, deg_done = (
                sem(n) for n in ("mask_ready", "trans_done", "stage_ready", "h0_ready", "h0T_ps", "h0T_ready", "h_ps",
                                 "h_copied", "ds_copied", "halved", "deg_done"))
            dg_ld = [sem(f"dg_ld{i}") for i in range(2)]
            dg_cast, dg_ps, dg_copied, dg_out = (sem(n) for n in ("dg_cast", "dg_ps", "dg_copied", "dg_out"))
            B_H0T, B_H, B_DS = 4, 5, 6

            def row(a, n):
                return a[:, bass.ds(n, 1), :].rearrange("p o f -> p (o f)")

            def diagonal(a, first, tiles):
                return bass.AP(tensor=a.tensor, offset=first * (P * N + P), ap=[[N, P], [P * N + P, tiles], [1, P]])

            with nc.Block() as block:
                @block.sync
                def _(sp):
                    sp.dma_start(Wl[:], W.rearrange("(c p) f -> p c f", p=P)).then_inc(w_in, 16)
                    n = NT // XP
                    for i in range(XP):
                        sp.dma_start(XH[:, i * n:(i + 1) * n, :],
                                     x[i * n * P:(i + 1) * n * P, :].rearrange("(t p) f -> p t f", p=P)).then_inc(x_in[i], 16)
                    for half in range(2):
                        sp.dma_start(dg_in[half], diagonal(adj, half * (NT // 2), NT // 2)).then_inc(dg_ld[half], 16)
                    with sp.Fori(0, NB1) as b:
                        for q in range(4):
                            sp.wait_ge(mask_ready, b * 4 + q + 1)
                            sp.dma_start(adj_in[:, q % 2],
                                         adj[bass.ds(b * IB1, IB1), q * JQ:(q + 1) * JQ].rearrange("(t p) c -> p t c", p=P)
                                         ).then_inc(adj_ld[q % 2], 16)

                @block.gpsimd
                def _(pool):
                    nc.gpsimd.memset(a_blk[:], 0.0).then_inc(a_cleared, 1)
                    nc.gpsimd.memset(identf[:], 0.0).then_inc(ident_set, 1)
                    nc.gpsimd.memset(identb[:], 0.0).then_inc(ident_set, 1)
                    nc.gpsimd.memset(identh[:], 0.0).then_inc(ident_set, 1)
                    pool.wait_ge(ident_set, 3)
                    for m in (identf, identb, identh):
                        nc.gpsimd.affine_select(out=m[:], in_=m[:], compare_op=ALU.not_equal, fill=1.0, base=0,
                                                pattern=[[-1, P]], channel_multiplier=1).then_inc(ident_set, 1)
                    pool.wait_ge(dg_copied, 2)
                    pool.dma_start(diag_raw, dg_T[:]).then_inc(dg_out, 16)
                    for i in range(2):
                        pool.wait_ge(stage_out[i], 16 * 2 * NB1 + 16)
                    pool.wait_ge(dg_out, 16)

                @block.vector
                def _(dve):
                    dve.sem_inc(mask_ready, 2)
                    dve.sem_inc(h_copied, 1)
                    dve.sem_inc(ds_copied, 1)
                    dve.wait_ge(a_cleared, 1)
                    dve.wait_ge(a_in, 32)
                    for i in range(2):
                        rows = slice(i * D, (i + 1) * D)
                        flat = a_blk[rows].rearrange("p c o -> p (c o)")
                        for k in range(2):
                            first, step = k * H + i, 2 * H + 2
                            nc.vector.tensor_copy(flat[:, first:first + (FC - 1) * step + 1:step], a_col[rows, k]).then_inc(a_set, 1)
                    dve.wait_ge(w_ps, 1)
                    nc.vector.tensor_copy(WT[:], PS[:, 0:FC, :]).then_inc(w_copied, 1)
                    for t in range(NT):
                        if t % (NT // XP) == 0:
                            dve.wait_ge(x_in[t // (NT // XP)], 16)
                        nc.vector.bn_stats(stats[:, t, :], XH[:, t, :]).then_inc(stats_done, 1)
                    for t in range(NT):
                        dve.wait_ge(stats_done, t + 1)
                        nc.vector.bn_aggr(mv[:, t, :], stats[:, t, :]).then_inc(stats_done, 1)
                    dve.wait_ge(stats_done, 2 * NT)
                    nc.vector.tensor_scalar(ve[:], mv[:, :, 1], EPS, None, ALU.add).then_inc(var_ready, 1)

                    step = [0]

                    def link(ins):
                        step[0] += 1
                        ins.then_inc(norm_ready, 1)
                        dve.wait_ge(norm_ready, step[0])

                    dve.wait_ge(sd_ready, 1)
                    link(nc.vector.reciprocal(rstd[:], sd[:]))
                    link(nc.vector.tensor_tensor(tmp[:], rstd[:], rstd[:], ALU.mult))
                    link(nc.vector.tensor_tensor(tmp[:], tmp[:], ve[:], ALU.mult))
                    link(nc.vector.tensor_scalar(tmp[:], tmp[:], -0.5, 1.5, ALU.mult, ALU.add))
                    link(nc.vector.tensor_tensor(rstd[:], rstd[:], tmp[:], ALU.mult))
                    link(nc.vector.scalar_tensor_tensor(out=nmr[:], in0=mv[:, :, 0], scalar=-1.0, in1=rstd[:],
                                                        op0=ALU.mult, op1=ALU.mult))
                    dve.wait_ge(w_ps, 2)
                    nc.vector.tensor_copy(Wa[:], PS[:, FC, 0:FC * 2 * H].rearrange("p (k h) -> p k h", k=FC)).then_inc(w_copied, 1)
                    for half in range(2):
                        dve.wait_ge(dg_ld[half], 16)
                        o = half * (NT // 2)
                        nc.vector.tensor_scalar(dg_bf[:, o:o + NT // 2, :], dg_in[half], 0.0, None, ALU.is_gt).then_inc(dg_cast, 1)
                    dve.wait_ge(dg_ps, 1)
                    v = PS[:, 0:NT // 8, :].bitcast(BF16).rearrange("p b (t c) -> p (b t) c", c=P)
                    nc.vector.tensor_copy(dg_T[:], v).then_inc(dg_copied, 1)
                    dve.wait_ge(dg_copied, 1)
                    nc.vector.tensor_tensor(dg_0[:], dg_T[:], identb[:].unsqueeze(1).to_broadcast([P, NT, P]),
                                            ALU.max).then_inc(dg_copied, 1)

                    def cast(b, q, e):
                        dve.wait_ge(adj_ld[q % 2], (e + q // 2 + 1) * 16)
                        dve.wait_ge(trans_done, (b * 4 + q + 1) * CB)
                        nc.vector.tensor_scalar(mask[:, q % 2], adj_in[:, q % 2], 0.0, None, ALU.is_gt).then_inc(mask_ready, 1)

                    def degrees(b, q):
                        n = b * 4 + q
                        dve.wait_ge(mask_ready, n + 3)
                        src = mask[:, q % 2]
                        for i, dst in enumerate((half1, half2, half3)):
                            w = JQ >> (i + 1)
                            nc.vector.tensor_tensor(dst[:], src[:, :, 0:w], src[:, :, w:2 * w], ALU.add).then_inc(halved, 1)
                            dve.wait_ge(halved, n * 3 + i + 1)
                            src = dst
                        nc.vector.tensor_reduce(degq[:, bass.ds(b * TI, TI), q:q + 1].rearrange("p t o -> p (t o)"),
                                                half3[:], AX.X, ALU.add).then_inc(deg_done, 1)

                    def products_out(b, q):
                        n = b * 4 + q
                        dve.wait_ge(h_ps, n + 1)
                        nc.vector.tensor_scalar(row(XH, n), PS[:, B_H, :], 1.0, None, ALU.mult).then_inc(h_copied, 1)
                        nc.vector.tensor_copy(row(d_s, n), PS[:, B_DS, 0:2 * H]).then_inc(ds_copied, 1)

                    def quarters(b, last):
                        for q in range(4):
                            if q < 3:
                                cast(b, q + 1, b * 2)
                            elif not last:
                                cast(b + 1, 0, b * 2 + 2)
                            degrees(b, q)
                            products_out(b, q)

                    cast(0, 0, 0)
                    with dve.Fori(0, NB1 - 1) as b:
                        quarters(b, False)
                    quarters(NB1 - 1, True)
                    dve.wait_ge(deg_done, 4 * NB1)
                    nc.vector.tensor_reduce(deg[:], degq[:], AX.X, ALU.add).then_inc(deg_done, 1)
                    dve.wait_ge(deg_done, 4 * NB1 + 1)
                    nc.vector.tensor_scalar(deg[:], deg[:], 1.0, GSCALE, ALU.max, ALU.mult).then_inc(deg_done, 1)
                    dve.wait_ge(deg_done, 4 * NB1 + 2)
                    nc.vector.reciprocal(rdeg[:], deg[:]).then_inc(deg_done, 1)

                @block.scalar
                def _(act):
                    with nc.allow_non_contiguous_dma(reason="columns of the attention vectors"):
                        for i, a in enumerate((a_dst, a_src)):
                            act.dma_start(a_col[:, i], a.rearrange("h d -> (h d)").rearrange("(c p) -> p c", p=P)).then_inc(a_in, 16)
                    act.wait_ge(var_ready, 1)
                    nc.scalar.activation(sd[:], ve[:], ACT.Sqrt).then_inc(sd_ready, 1)
                    act.wait_ge(norm_ready, 6)
                    act.sem_inc(stage_ready, CB)
                    act.sem_inc(h0T_ready, 1)
                    for i in range(2):
                        act.sem_inc(stage_out[i], 16)
                    with act.Fori(0, NB1) as b:
                        for q in range(4):
                            n = b * 4 + q
                            act.wait_ge(h0T_ps, n + 1)
                            nc.scalar.activation(h0[:, q % 2], row(XH, n), ACT.Relu,
                                                 bias=nmr[:, bass.ds(n, 1)], scale=rstd[:, bass.ds(n, 1)]).then_inc(h0_ready, 1)
                            act.wait_ge(h0T_ps, n + 3)
                            nc.scalar.activation(h0T[:, q % 2], PS[:, B_H0T, :].rearrange("p (k c) -> p k c", k=FC),
                                                 ACT.Copy).then_inc(h0T_ready, 1)
                            act.wait_ge(stage_out[q % 2], (b * 2 + q // 2 + 1) * 16)
                            for c in range(CB):
                                act.wait_ge(trans_done, (n + 2) * CB + c + 1)
                                nc.scalar.activation(stage[:, q % 2, 2 * c:2 * c + 2, :],
                                                     bank16(c, BF16).rearrange("p (t i) -> p t i", t=2), ACT.Copy).then_inc(stage_ready, 1)
                            act.wait_ge(stage_ready, (n + 2) * CB)
                            act.dma_start(maskT[q * JQ:(q + 1) * JQ, bass.ds(b * IB1, IB1)].rearrange("(t p) c -> p t c", p=P),
                                          stage[:, q % 2]).then_inc(stage_out[q % 2], 16)

                @block.tensor
                def _(pe):
                    pe.wait_ge(ident_set, 6)
                    pe.wait_ge(w_in, 16)
                    for k in range(FC):
                        for c in range(FC):
                            last = nc.tensor.transpose(PS[:, k, c * P:(c + 1) * P], Wl[:, c, k * P:(k + 1) * P], identf[:])
                    last.then_inc(w_ps, 1)
                    pe.wait_ge(a_set, 4)
                    for k in range(FC):
                        for c in range(FC):
                            last = nc.tensor.matmul(PS[:, FC, k * 2 * H:(k + 1) * 2 * H], Wl[:, c, k * P:(k + 1) * P], a_blk[:, c, :],
                                                    start=c == 0, stop=c == FC - 1)
                    last.then_inc(w_ps, 1)
                    pe.sem_inc(trans_done, 2 * CB)
                    pe.sem_inc(h0T_ps, 2)
                    pe.wait_ge(w_copied, 2)
                    pe.wait_ge(dg_cast, 2)
                    for t in range(NT):
                        last = nc.tensor.transpose(bank16(t // 8, BF16)[:, (t % 8) * P:(t % 8 + 1) * P], dg_bf[:, t, :], identb[:])
                    last.then_inc(dg_ps, 1)
                    pe.wait_ge(dg_copied, 1)
                    with pe.Fori(0, NB1) as b:
                        for q in range(4):
                            n = b * 4 + q
                            pe.wait_ge(mask_ready, n + 3)
                            for c in range(CB):
                                pe.wait_ge(stage_ready, n * CB + c + 1)
                                for k in range(2):
                                    for ti in range(TI):
                                        o = (k * TI + ti) * P
                                        last = nc.tensor.transpose(bank16(c, BF16)[:, o:o + P],
                                                                   mask[:, q % 2, ti, (2 * c + k) * P:(2 * c + k + 1) * P], identb[:])
                                last.then_inc(trans_done, 1)
                            pe.wait_ge(h0_ready, n + 1)
                            pe.wait_ge(h0T_ready, n + 1)
                            for k in range(FC):
                                last = nc.tensor.transpose(PS[:, B_H0T, k * P:(k + 1) * P], h0[:, q % 2, k * P:(k + 1) * P], identf[:])
                            last.then_inc(h0T_ps, 1)
                            pe.wait_ge(h_copied, n + 1)
                            pe.wait_ge(ds_copied, n + 1)
                            pe.wait_ge(h0T_ready, n + 2)
                            for k in range(FC):
                                nc.tensor.matmul(PS[:, B_H, :], h0T[:, q % 2, k, :], WT[:, k, :], start=k == 0, stop=k == FC - 1)
                            for k in range(FC):
                                last = nc.tensor.matmul(PS[:, B_DS, 0:2 * H], h0T[:, q % 2, k, :], Wa[:, k, :],
                                                        start=k == 0, stop=k == FC - 1)
                            last.then_inc(h_ps, 1)

        with ExitStack() as ctx:
            bp = sb(ctx, "bp", [P, H, NT], F32)
            bm = sb(ctx, "bm", [P, H, NT], F32)
            dc = sb(ctx, "dc", [P, H, NT], F32)
            t_i = sb(ctx, "t_i", [P, H, NT], F32)
            lk = sb(ctx, "lk", [P, H, NT], F32)
            dmax = sb(ctx, "dmax", [P, H], F32)
            dall = sb(ctx, "dall", [P, H], F32)
            s_T = sb(ctx, "s_T", [NT, H, P], F32)
            val = sb(ctx, "val", [P, 2, 2, NT, DE], F32)
            Wp = sb(ctx, "Wp", [P, FC, F], F32)
            WpT = sb(ctx, "WpT", [P, FC, F], F32)
            Wc = sb(ctx, "Wc", [P, FC, F], F32)
            bcol = sb(ctx, "bcol", [P, 2 * FC], F32)
            bwide = sb(ctx, "bwide", [P, 2 * FC, P], F32)
            bc_row = sb(ctx, "bc_row", [P, F], F32)
            sb(ctx, "clear", [P, 256], F32)
            parts = sb(ctx, "parts", [P, 2, NT, VALW], BF16)
            dmax_ready, dall_ready, small, exp_done, sT_ps, sT_ready, s_out = (
                sem(n) for n in ("dmax_ready", "dall_ready", "small", "exp_done", "sT_ps", "sT_ready", "s_out"))
            val_ready, hi_ready, rest_ready, mid_ready, minus_ready, plus_ready = (
                sem(n) for n in ("val_ready", "hi_ready", "rest_ready", "mid_ready", "minus_ready", "plus_ready"))
            parts_out = [sem(f"parts_out{i}") for i in range(2)]
            b_in, wide, fused_ps, fused_copied, w_lo_ready = (sem(n) for n in ("b_in", "wide", "fused_ps", "fused_copied", "w_lo_ready"))
            wp_in = [sem(f"wp_in{i}") for i in range(2)]
            wc_in = [sem(f"wc_in{i}") for i in range(2)]
            B_W, B_BIAS = 2, 7
            d_v = d_s[:, :, 0:H].rearrange("p t h -> p h t")
            s_v = d_s[:, :, H:2 * H].rearrange("p t h -> p h t")
            dall_b = dall[:].unsqueeze(2).to_broadcast([P, H, NT])

            def part(e, i):
                p = parts[:, e, :, i * DE:(i + 1) * DE]
                return p if i < PP else p.bitcast(FP16)

            with nc.Block() as block:
                @block.sync
                def _(sp):
                    for e in range(2):
                        sp.sem_inc(parts_out[e], 16)
                    sp.dma_start(Wp[:], W_self.rearrange("(c p) f -> p c f", p=P)).then_inc(wp_in[0], 16)
                    sp.dma_start(Wc[:], W_comb[0:F, :].rearrange("(c p) f -> p c f", p=P)).then_inc(wc_in[0], 16)
                    sp.wait_ge(sT_ready, 1)
                    for b in range(NB):
                        sp.dma_start(s_rows[b].rearrange("h (k p) -> k h p", p=P), s_T[b * KB:(b + 1) * KB]).then_inc(s_out, 16)
                    for h in range(H - 1):
                        if h == 1:
                            sp.wait_ge(fused_ps, 1)
                            sp.dma_start(Wp[:], W_nb.rearrange("(c p) f -> p c f", p=P)).then_inc(wp_in[1], 16)
                        if h == 3:
                            sp.wait_ge(fused_ps, 2)
                            sp.dma_start(Wc[:], W_comb[F:2 * F, :].rearrange("(c p) f -> p c f", p=P)).then_inc(wc_in[1], 16)
                        sp.wait_ge(minus_ready, h + 1)
                        sp.wait_ge(plus_ready, h + 3)
                        sp.dma_start(vals[h], parts[:, h % 2]).then_inc(parts_out[h % 2], 16)
                    sp.wait_ge(parts_out[0], 16 + 16 * (H // 2))
                    sp.wait_ge(parts_out[1], 16 * (H // 2))
                    sp.wait_ge(s_out, 16 * NB)
                    sp.wait_ge(dg_out, 32)

                @block.gpsimd
                def _(pool):
                    pool.sem_inc(plus_ready, 2)
                    pool.dma_start(diagonal(maskT, 0, NT), dg_0).then_inc(dg_out, 16)
                    with nc.allow_non_contiguous_dma(reason="bias columns"):
                        pool.dma_start(bcol[:, 0:FC], b_self.rearrange("(c p) -> p c", p=P)).then_inc(b_in, 16)
                        pool.dma_start(bcol[:, FC:], b_nb.rearrange("(c p) -> p c", p=P)).then_inc(b_in, 16)
                    pool.dma_start(bc_row[:], b_comb.rearrange("(o f) -> o f", o=1).to_broadcast([P, F])).then_inc(b_in, 16)
                    pool.wait_ge(dmax_ready, 1)
                    nc.gpsimd.partition_all_reduce(dall[:], dmax[:], P, RMAX).then_inc(dall_ready, 1)
                    pool.wait_ge(b_in, 48)
                    nc.gpsimd.tensor_copy(bwide[:], bcol[:].unsqueeze(2).to_broadcast([P, 2 * FC, P])).then_inc(wide, 1)
                    with pool.Fori(0, H // 2) as hp:
                        for e in range(2):
                            pool.wait_ge(mid_ready, hp * 2 + e + 1)
                            nc.gpsimd.tensor_tensor(part(e, 2), val[:, e, 0], part(e, 1), ALU.subtract).then_inc(plus_ready, 1)

                @block.tensor
                def _(pe):
                    for h in range(H):
                        last = nc.tensor.transpose(PS[0:NT, h // 4, (h % 4) * P:(h % 4 + 1) * P], d_s[:, :, H + h], identf[:])
                    last.then_inc(sT_ps, 1)
                    for i in range(2):
                        pe.wait_ge(wp_in[i], 16)
                        if i:
                            pe.wait_ge(fused_copied, 2)
                            pe.wait_ge(w_lo_ready, 1)
                        for k in range(FC):
                            for c in range(FC):
                                last = nc.tensor.transpose(PS[:, B_W + k, c * P:(c + 1) * P], Wp[:, c, k * P:(k + 1) * P], identf[:])
                        last.then_inc(fused_ps, 1)
                        pe.wait_ge(wc_in[i], 16)
                        pe.wait_ge(wide, 1)
                        for c in range(FC):
                            nc.tensor.matmul(PS[:, B_BIAS, :], bwide[:, i * FC + c, :], Wc[:, c, :],
                                             start=i == 0 and c == 0, stop=i == 1 and c == FC - 1)
                        pe.wait_ge(fused_copied, 2 * i + 1)
                        for k in range(FC):
                            for c in range(FC):
                                last = nc.tensor.matmul(PS[:, B_W + k, :], WpT[:, c, k * P:(k + 1) * P], Wc[:, c, :],
                                                        start=c == 0, stop=c == FC - 1)
                        last.then_inc(fused_ps, 1)

                @block.vector
                def _(dve):
                    step = [0]

                    def link(ins):
                        step[0] += 1
                        ins.then_inc(small, 1)
                        dve.wait_ge(small, step[0])

                    nc.vector.tensor_reduce(dmax[:], d_v, AX.X, ALU.max).then_inc(dmax_ready, 1)
                    for b in range(NB):
                        nc.vector.tensor_scalar(bias_j[:, b], d_v, BIG, None, ALU.mult)
                    dve.wait_ge(sT_ps, 1)
                    nc.vector.tensor_scalar(s_T[:], PS[0:NT, 0:2, :].rearrange("t b (h p) -> t (b h) p", p=P), BIG, None,
                                            ALU.mult).then_inc(sT_ready, 1)
                    dve.wait_ge(dall_ready, 1)
                    link(nc.vector.tensor_tensor(dc[:], d_v, dall_b, ALU.subtract))
                    link(nc.vector.tensor_tensor(t_i[:], s_v, dall_b, ALU.add))
                    link(nc.vector.scalar_tensor_tensor(out=lk[:], in0=t_i[:], scalar=SLOPE, in1=t_i[:], op0=ALU.mult, op1=ALU.max))
                    link(nc.vector.tensor_tensor(a_i[:], t_i[:], lk[:], ALU.subtract))
                    link(nc.vector.scalar_tensor_tensor(out=c_i[:], in0=t_i[:], scalar=SLOPE, in1=lk[:], op0=ALU.mult,
                                                        op1=ALU.subtract))
                    dve.wait_ge(exp_done, 4)
                    link(nc.vector.tensor_scalar(bm[:], bm[:], MSCALE, None, ALU.mult))
                    link(nc.vector.tensor_scalar(c_i[:], c_i[:], 1.0 / MSCALE, None, ALU.mult))
                    def two_heads(hp, w):
                        def value(e, s):
                            b_ = (bp, bm)[s][:, bass.ds(hp * 2 + e, 1), :].rearrange("p o t -> p (o t)")
                            nc.vector.tensor_tensor(val[:, e, s, :, 0:D], XH[:, :, bass.ds((hp * 2 + e) * D, D)],
                                                    b_.unsqueeze(2).to_broadcast([P, NT, D]), ALU.mult)
                            nc.vector.tensor_copy(val[:, e, s, :, D:DE], b_.unsqueeze(2)).then_inc(val_ready, 1)

                        def rest(e):
                            dve.wait_ge(hi_ready, hp * 4 + e * 2 + 1)
                            nc.vector.tensor_tensor(val[:, e, 0], val[:, e, 0], part(e, 0), ALU.subtract).then_inc(rest_ready, 1)

                        def minus_rest(e):
                            dve.wait_ge(hi_ready, hp * 4 + e * 2 + 2)
                            nc.vector.tensor_tensor(part(e, 4), val[:, e, 1], part(e, 3), ALU.subtract).then_inc(minus_ready, 1)

                        dve.wait_ge(plus_ready, hp * 2 + 1)
                        value(0, 0)
                        value(0, 1)
                        if w is not None:
                            weights_rest(w)
                        rest(0)
                        dve.wait_ge(plus_ready, hp * 2 + 2)
                        value(1, 0)
                        minus_rest(0)
                        value(1, 1)
                        rest(1)
                        minus_rest(1)

                    def weights_rest(i):
                        dve.wait_ge(fused_copied, 2 * i + 2)
                        ks = slice(i * FC, (i + 1) * FC)
                        nc.vector.scalar_tensor_tensor(out=w_parts[:, ks, 1, :], in0=PS[:, B_W:B_W + FC, :], scalar=WSCALE,
                                                       in1=w_parts[:, ks, 0, :], op0=ALU.mult, op1=ALU.subtract).then_inc(w_lo_ready, 1)

                    with dve.Fori(0, H // 4) as hp:
                        two_heads(hp, None)
                    two_heads(H // 4, 0)
                    for hp in range(H // 4 + 1, H // 2):
                        two_heads(hp, None)
                    weights_rest(1)
                    dve.wait_ge(fused_copied, 5)
                    nc.vector.tensor_tensor(bias_row, bias_row, bc_row[:], ALU.add).then_inc(wide, 1)

                @block.scalar
                def _(act):
                    def copied(dst, b0, banks, done, scale=1.0):
                        act.wait_ge(fused_ps, done)
                        nc.scalar.activation(dst, PS[:, b0:b0 + banks, :], ACT.Copy, scale=scale).then_inc(fused_copied, 1)

                    act.wait_ge(small, 1)
                    nc.scalar.activation(bp[:], dc[:], ACT.Exp).then_inc(exp_done, 1)
                    nc.scalar.activation(bm[:], dc[:], ACT.Exp, scale=SLOPE).then_inc(exp_done, 1)
                    act.wait_ge(small, 5)
                    nc.scalar.activation(a_i[:], a_i[:], ACT.Exp).then_inc(exp_done, 1)
                    nc.scalar.activation(c_i[:], c_i[:], ACT.Exp).then_inc(exp_done, 1)
                    for hp in range(H // 2):
                        def hi(e, s):
                            act.wait_ge(val_ready, hp * 4 + e * 2 + s + 1)
                            nc.scalar.activation(part(e, s * PP), val[:, e, s], ACT.Copy).then_inc(hi_ready, 1)

                        def mid(e):
                            act.wait_ge(rest_ready, hp * 2 + e + 1)
                            nc.scalar.activation(part(e, 1), val[:, e, 0], ACT.Copy).then_inc(mid_ready, 1)

                        act.wait_ge(parts_out[0], (hp + 1) * 16)
                        hi(0, 0)
                        hi(0, 1)
                        mid(0)
                        act.wait_ge(parts_out[1], (hp + 1) * 16)
                        hi(1, 0)
                        hi(1, 1)
                        mid(1)
                        i = hp // 2
                        if hp == 1:
                            act.wait_ge(dg_out, 32)
                        if hp % 2 == 0:
                            copied(WpT[:], B_W, FC, 2 * i + 1)
                        else:
                            copied(w_parts[:, i * FC:(i + 1) * FC, 0, :], B_W, FC, 2 * i + 2, WSCALE)
                    copied(bias_row.unsqueeze(1), B_BIAS, 1, 4)

        m1_ld = [whole.enter_context(nc.semaphore(f"m1_ld{i}")) for i in range(2)]
        m1_dg = [whole.enter_context(nc.semaphore(f"m1_dg{i}")) for i in range(2)]

        def load_mask(sp, m1_, e, b, count):
            sp.dma_start(m1_[:], maskT[:, bass.ds(b * IB1, IB1)].rearrange("(t p) i -> p t i", p=P)).then_inc(m1_ld[e], 16)
            sp.wait_ge(m1_ld[e], count * 16)
            for ti in range(TI):
                sp.dma_start(m1_[:, bass.ds(b * TI + ti, 1), ti * P:(ti + 1) * P],
                             diag_raw[:, bass.ds(b * TI + ti, 1), :]).then_inc(m1_dg[e], 16)

        x_ld = [sem(f"x_ld{i}") for i in range(2)]
        at_ld = [sem(f"at_ld{i}") for i in range(2)]

        def load_x(sp, b, e):
            sp.dma_start(x1[:, e], x[bass.ds(b * IB, IB), :].rearrange("(k p) f -> p k f", p=P)).then_inc(x_ld[e], 16)

        def load_attention(sp, b, e):
            sp.dma_start(at[:, e].rearrange("p h k d -> p h (k d)"),
                         attn[bass.ds(b, 1)].rearrange("o h p c -> (o p) h c")).then_inc(at_ld[e], 16)

        R = NB * H
        with ExitStack() as ctx:
            minus1 = sb(ctx, "minus1", [P, KB], F32)
            vt = sb(ctx, "vt", [P, NT, VALW], BF16)
            srow = sb(ctx, "srow", [P, 2, IB], F32)
            stp = sb(ctx, "stp", [P, RS, G, IB], BF16)
            mp = sb(ctx, "mp", [P, RM, G, IB], BF16)
            mm = sb(ctx, "mm", [P, RM, G, IB], BF16)
            acc = sb(ctx, "acc", [P, KB, PP + PM, DE], F32)
            whole_s = sb(ctx, "whole_s", [P, KB, 2, DE], F32)
            joined = sb(ctx, "joined", [P, KB, DE], F32)
            rden = sb(ctx, "rden", [P, KB], F32)
            o_sb = sb(ctx, "o_sb", [P, KB, D], F32)

            mt_ld = [sem(f"mt_ld{i}") for i in range(2)]
            vt_ld = [sem(f"vt_ld{i}") for i in range(2)]
            srow_ld, srow_used, step_ready, mp_ready, mm_ready, bank_done, acc_ready, acc_free, join, o_out, set_up = (
                sem(n) for n in ("srow_ld", "srow_used", "step_ready", "mp_ready", "mm_ready", "bank_done",
                                 "acc_ready", "acc_free", "join", "o_out", "set_up"))
            ROUND = NG * KB
            JOIN = 7
            bias_f = bias_j[:].rearrange("p b h t -> p (b h t)")

            with nc.Block() as block:
                @block.sync
                def _(sp):
                    def load_srow(b, h):
                        r = b * H + h
                        sp.wait_ge(srow_ld, (r + 1) * 16)
                        sp.wait_ge(srow_used, r + 1)
                        sp.dma_start(srow[:, bass.ds(r % 2, 1)].rearrange("p o i -> p (o i)"),
                                     s_rows[bass.ds(b, 1), bass.ds(h, 1)].rearrange("o q i -> (o q) i").to_broadcast([P, IB])
                                     ).then_inc(srow_ld, 16)

                    def load_groups(b, h, with_mask):
                        r = b * H + h
                        for l in range(NL):
                            js = slice(l * LG, (l + 1) * LG)
                            sp.wait_ge(bank_done, r * ROUND + (l + 1) * (LG // G) * KB)
                            sp.wait_ge(vt_ld[l % 2], (r * (NL // 2) + l // 2 + 1) * 16)
                            sp.dma_start(vt[:, js, :], vals[bass.ds(h, 1), :, js, :].rearrange("o p t c -> (o p) t c")
                                         ).then_inc(vt_ld[l % 2], 16)
                            if with_mask:
                                sp.wait_ge(mt_ld[l % 2], (b * (NL // 2) + l // 2 + 1) * 16)
                                sp.dma_start(mt[:, js, :], maskT[l * LG * P:(l + 1) * LG * P, bass.ds(b * IB, IB)]
                                             .rearrange("(t p) i -> p t i", p=P)).then_inc(mt_ld[l % 2], 16)

                    for ld in (srow_ld, *vt_ld, *mt_ld):
                        sp.sem_inc(ld, 16)
                    with sp.Fori(0, NB) as b:
                        load_srow(b, 0)
                        load_groups(b, 0, True)
                        sp.wait_ge(parts_out[1], 16 + 16 * (H // 2))
                        with sp.Fori(1, H) as h:
                            load_srow(b, h)
                            load_groups(b, h, False)
                    sp.wait_ge(mm_ready, R * NG)
                    load_x(sp, 0, 0)
                    load_attention(sp, 0, 0)

                @block.scalar
                def _(act):
                    act.sem_inc(srow_used, 2)
                    act.sem_inc(acc_ready, KB)

                    def steps(r, c):
                        for u in range(RS):
                            act.wait_ge(mp_ready, r * NG + c * RS + u + 1)
                            for j in range(G):
                                last = nc.scalar.activation(stp[:, u, j, :], srow[:, bass.ds(r % 2, 1)].rearrange("p o i -> p (o i)"),
                                                            ACT.Relu, bias=bias_f[:, bass.ds(r * NT + c * (RS * G) + u * G + j, 1)])
                            last.then_inc(step_ready, 1)

                    def copy_out(r):
                        act.wait_ge(acc_free, r + 1)
                        for k in range(KB):
                            act.wait_ge(bank_done, (r + 2) * ROUND - KB + k + 1)
                            nc.scalar.activation(acc[:, k].rearrange("p q c -> p (q c)"), PS[:, k, 0:VALW],
                                                 ACT.Copy).then_inc(acc_ready, 1)

                    def store(r):
                        act.wait_ge(join, (r + 1) * JOIN)
                        act.dma_start(attn.rearrange("b h p c -> (b h) p c")[bass.ds(r, 1)].rearrange("o p c -> (o p) c"),
                                      o_sb[:].rearrange("p k c -> p (k c)")).then_inc(o_out, 16)

                    act.sem_inc(o_out, 16)
                    act.wait_ge(srow_ld, 32)
                    steps(0, 0)
                    act.dma_start(vals[H - 1], parts[:, 1]).then_inc(parts_out[1], 16)
                    with act.Fori(1, NG // RS) as c:
                        steps(0, c)
                    act.wait_ge(parts_out[1], 16 + 16 * (H // 2))
                    with act.Fori(1, R) as r:
                        act.wait_ge(srow_ld, (r + 2) * 16)
                        steps(r, 0)
                        act.wait_ge(step_ready, r * NG)
                        act.sem_inc(srow_used, 1)
                        copy_out(r - 1)
                        with act.Fori(1, NG // RS) as c:
                            steps(r, c)
                        store(r - 1)
                    copy_out(R - 1)
                    store(R - 1)
                    act.wait_ge(o_out, (R + 1) * 16)

                @block.vector
                def _(dve):
                    dve.sem_inc(mp_ready, RS)
                    with dve.Fori(0, NB) as b:
                        with dve.Fori(0, H) as h:
                            with dve.Fori(0, NG // RS) as c:
                                def group(u):
                                    return (b * H + h) * NG + c * RS + u, mt[:, bass.ds(c * (RS * G) + u * G, G), :]

                                def plus(u):
                                    n, m_ = group(u)
                                    l = u * G // LG
                                    dve.wait_ge(step_ready, n + 1)
                                    dve.wait_ge(mt_ld[l % 2], (b * (NL // 2) + c * (RS * G // LG // 2) + l // 2 + 2) * 16)
                                    dve.wait_ge(bank_done, ROUND - (RM - 1) * KB + n * KB)
                                    nc.vector.tensor_tensor(mp[:, u % RM], stp[:, u], m_, ALU.min).then_inc(mp_ready, 1)

                                def minus(u):
                                    n, m_ = group(u)
                                    dve.wait_ge(mp_ready, n + RS + 1)
                                    nc.vector.tensor_tensor(mm[:, u % RM], m_, mp[:, u % RM], ALU.subtract).then_inc(mm_ready, 1)

                                for u in range(0, RS, 2):
                                    plus(u)
                                    plus(u + 1)
                                    minus(u)
                                    minus(u + 1)

                @block.tensor
                def _(pe):
                    pe.sem_inc(bank_done, ROUND)

                    def group(r, c, u, opens):
                        l = u * G // LG
                        pe.wait_ge(vt_ld[l % 2], (r * (NL // 2) + c * (RM * G // LG // 2) + l // 2 + 2) * 16)
                        pe.wait_ge(mm_ready, r * NG + c * RM + u + 1)
                        for k in range(KB):
                            if opens:
                                pe.wait_ge(acc_ready, r * KB + k + 1)
                            for j in range(G):
                                v = vt[:, bass.ds(c * (RM * G) + u * G + j, 1), :].rearrange("p o c -> p (o c)")
                                first = opens and j == 0
                                nc.tensor.matmul(PS[:, k, 0:VP], mp[:, u, j, k * P:(k + 1) * P], v[:, 0:VP],
                                                 start=first, stop=not first, skip_group_check=True)
                                last = nc.tensor.matmul(PS[:, k, VP:VALW], mm[:, u, j, k * P:(k + 1) * P], v[:, VP:VALW].bitcast(FP16),
                                                        start=False, stop=True, skip_group_check=True)
                            last.then_inc(bank_done, 1)

                    with pe.Fori(0, R) as r:
                        for u in range(RM):
                            group(r, 0, u, u == 0)
                        with pe.Fori(1, NG // RM) as c:
                            for u in range(RM):
                                group(r, c, u, False)

                @block.gpsimd
                def _(pool):
                    nc.gpsimd.memset(minus1[:], -1.0).then_inc(set_up, 1)
                    pool.wait_ge(set_up, 1)
                    pool.sem_inc(acc_free, 1)
                    with pool.Fori(0, NB) as b:
                        with pool.Fori(0, H) as h:
                            r = b * H + h

                            def step(n, ins):
                                ins.then_inc(join, 1)
                                pool.wait_ge(join, r * JOIN + n)

                            def rows_of(c):
                                return c[:, bass.ds(h, 1), bass.ds(b * KB, KB)].rearrange("p o k -> p (o k)").unsqueeze(2) \
                                    .to_broadcast([P, KB, DE])

                            pool.wait_ge(acc_ready, (r + 2) * KB)
                            step(1, nc.gpsimd.tensor_tensor(whole_s[:], acc[:, :, 0:PP + 1:PP, :], acc[:, :, 1:PP + 2:PP, :], ALU.add))
                            step(2, nc.gpsimd.tensor_tensor(whole_s[:, :, 0, :], whole_s[:, :, 0, :], acc[:, :, 2, :], ALU.add))
                            pool.sem_inc(acc_free, 1)
                            step(3, nc.gpsimd.tensor_tensor(whole_s[:, :, 0, :], whole_s[:, :, 0, :], rows_of(a_i), ALU.mult))
                            step(4, nc.gpsimd.tensor_tensor(whole_s[:, :, 1, :], whole_s[:, :, 1, :], rows_of(c_i), ALU.mult))
                            step(5, nc.gpsimd.tensor_tensor(joined[:], whole_s[:, :, 0, :], whole_s[:, :, 1, :], ALU.add))
                            step(6, nc.gpsimd.tensor_tensor(rden[:], joined[:, :, D], minus1[:], ALU.pow))
                            pool.wait_ge(o_out, (r + 1) * 16)
                            step(7, nc.gpsimd.tensor_tensor(o_sb[:], joined[:, :, 0:D], rden[:].unsqueeze(2).to_broadcast([P, KB, D]),
                                                            ALU.mult))

        layer1 = ExitStack()
        gh = sb(layer1, "gh", [P, NT, F], FP16)
        gl = sb(layer1, "gl", [P, NT, F], FP16)
        m1a = sb(layer1, "m1a", [P, NT, IB1], BF16)

        with ExitStack() as ctx:
            UNSCALE = 1.0 / (HSCALE * WSCALE)
            h1 = sb(ctx, "h1", [P, 2, F], F32)
            h1_parts = sb(ctx, "h1_parts", [P, 2, 2, F], FP16)
            h1T = sb(ctx, "h1T", [P, 2, 2 * FC, P], FP16)
            sf = sb(ctx, "sf", [P, 2, F], F32)
            stats1 = sb(ctx, "stats1", [P, KB, 6], F32)
            mv1 = sb(ctx, "mv1", [P, KB, 2], F32)
            ve1, sd1, tmp1 = (sb(ctx, n, [P, KB], F32) for n in ("ve1", "sd1", "tmp1"))
            gate = sb(ctx, "gate", [P, 1], F32)
            rstd1 = sb(ctx, "rstd1", [P, 2, KB], F32)
            nmr1 = sb(ctx, "nmr1", [P, 2, KB], F32)

            x1_ready, st1, sd1_ready, ln_ready, h1_ready, h1_lo_ready, hT_ps, hT_ready, both_ps, self_ready, gh_ready, gl_ready = (
                sem(n) for n in ("x1_ready", "st1", "sd1_ready", "ln_ready", "h1_ready", "h1_lo_ready", "hT_ps", "hT_ready",
                                 "both_ps", "self_ready", "gh_ready", "gl_ready"))
            x1_out = [sem(f"x1_out{i}") for i in range(2)]
            sf_out = [sem(f"sf_out{i}") for i in range(2)]
            LN = 7
            PAIR = 2 * KB
            NPAIR = NB // 2

            with nc.Block() as block:
                @block.sync
                def _(sp):
                    def store(b, bp, e, more):
                        sp.wait_ge(x1_ready, (b + 1) * KB)
                        sp.dma_start(x1_self[bass.ds(b * KB, KB), :, 0, :].rearrange("k p f -> p k f"), x1[:, e]).then_inc(x1_out[e], 16)
                        if more:
                            load_attention(sp, b + 2, e)
                        for k in range(KB):
                            if more and k == KB - 2:
                                sp.wait_ge(h1_ready, (b + 1) * KB)
                                sp.wait_ge(x1_out[e], (bp + 2) * 16)
                                load_x(sp, b + 2, e)
                            sp.wait_ge(self_ready, 2 + b * KB + k + 1)
                            sp.dma_start(x1_self[bass.ds(b * KB + k, 1), :, 1, :].rearrange("o p f -> (o p) f"),
                                         sf[:, k % 2]).then_inc(sf_out[k % 2], 16)

                    for e in range(2):
                        sp.sem_inc(x1_out[e], 16)
                        sp.sem_inc(sf_out[e], 16)
                    load_x(sp, 1, 1)
                    load_attention(sp, 1, 1)
                    load_mask(sp, m1a, 0, 0, 1)
                    with sp.Fori(0, NPAIR - 1) as bp:
                        for e in range(2):
                            store(bp * 2 + e, bp, e, True)
                    for e in range(2):
                        store(NB - 2 + e, NPAIR - 1, e, False)
                    for e in range(2):
                        sp.wait_ge(x1_out[e], 16 * NPAIR + 16)
                        sp.wait_ge(sf_out[e], 16 * NT // 2 + 16)

                @block.vector
                def _(dve):
                    def residual(b, bp, e, k):
                        if k == 0:
                            dve.wait_ge(x_ld[e], (bp + 1) * 16)
                            dve.wait_ge(at_ld[e], (bp + 1) * 16)
                        nc.vector.tensor_tensor(x1[:, e, k].rearrange("p (h d) -> p h d", d=D),
                                                x1[:, e, k].rearrange("p (h d) -> p h d", d=D),
                                                at[:, e, :, k, :], ALU.add).then_inc(x1_ready, 1)
                        dve.wait_ge(x1_ready, b * KB + k + 1)
                        nc.vector.bn_stats(stats1[:, k], x1[:, e, k]).then_inc(st1, 1)

                    def coefficients(b, e, k0=0, k1=KB):
                        ks = slice(k0, k1)
                        call = b + 1 if (k0, k1) == (0, KB) else k0 // (KB // 2)
                        dve.wait_ge(st1, b * 2 * KB + k0 + k1)
                        nc.vector.memset(gate[:], 0.0)
                        for k in range(k0, k1):
                            nc.vector.bn_aggr(mv1[:, k], stats1[:, k]).then_inc(st1, 1)
                        dve.wait_ge(st1, b * 2 * KB + 2 * k1)

                        def ln(n, ins):
                            ins.then_inc(ln_ready, 1)
                            dve.wait_ge(ln_ready, call * LN + n)

                        ln(1, nc.vector.tensor_scalar(ve1[:, ks], mv1[:, ks, 1], EPS, None, ALU.add))
                        dve.wait_ge(sd1_ready, call + 1)
                        rs = rstd1[:, e, ks]
                        ln(2, nc.vector.reciprocal(rs, sd1[:, ks]))
                        ln(3, nc.vector.tensor_tensor(tmp1[:, ks], rs, rs, ALU.mult))
                        ln(4, nc.vector.tensor_tensor(tmp1[:, ks], tmp1[:, ks], ve1[:, ks], ALU.mult))
                        ln(5, nc.vector.tensor_scalar(tmp1[:, ks], tmp1[:, ks], -0.5 * HSCALE, 1.5 * HSCALE, ALU.mult, ALU.add))
                        ln(6, nc.vector.tensor_tensor(rs, rs, tmp1[:, ks], ALU.mult))
                        ln(7, nc.vector.scalar_tensor_tensor(out=nmr1[:, e, ks], in0=mv1[:, ks, 0], scalar=-1.0, in1=rs,
                                                             op0=ALU.mult, op1=ALU.mult))

                    def products_out(b, k):
                        t = b * KB + k
                        dve.wait_ge(both_ps, t + 3)
                        dve.wait_ge(sf_out[k % 2], (b * (KB // 2) + k // 2 + 1) * 16)
                        nc.vector.scalar_tensor_tensor(out=sf[:, k % 2], in0=PS[:, 2 + k % 2, :], scalar=UNSCALE, in1=bias_row,
                                                       op0=ALU.mult, op1=ALU.add).then_inc(self_ready, 1)
                        dve.wait_ge(gh_ready, t + 1)
                        nc.vector.scalar_tensor_tensor(out=gl[:, bass.ds(t, 1)].rearrange("p o f -> p (o f)"), in0=PS[:, 4 + k % 2, :],
                                                       scalar=GSCALE * UNSCALE, in1=gh[:, bass.ds(t, 1)].rearrange("p o f -> p (o f)"),
                                                       op0=ALU.mult, op1=ALU.subtract).then_inc(gl_ready, 1)

                    def h1_rest(t, k):
                        dve.wait_ge(h1_ready, t + 1)
                        dve.wait_ge(hT_ps, t + 1)
                        nc.vector.tensor_tensor(h1_parts[:, k % 2, 1], h1[:, k % 2], h1_parts[:, k % 2, 0],
                                                ALU.subtract).then_inc(h1_lo_ready, 1)

                    def tiles(b, bp, e, ahead):
                        for k in range(KB):
                            if ahead and k < KB // 2:
                                residual(b + 1, bp + e, 1 - e, 2 * k)
                                residual(b + 1, bp + e, 1 - e, 2 * k + 1)
                            if ahead and k == KB // 2:
                                coefficients(b + 1, 1 - e)
                            if ahead or k < KB - 2:
                                h1_rest(b * KB + k + 2, k)
                            products_out(b, k)

                    dve.sem_inc(self_ready, 2)
                    dve.sem_inc(gl_ready, 2)
                    for k0 in (0, KB // 2):
                        for k in range(k0, k0 + KB // 2):
                            residual(0, 0, 0, k)
                        coefficients(0, 0, k0, k0 + KB // 2)
                        if k0 == 0:
                            h1_rest(0, 0)
                            h1_rest(1, 1)
                    with dve.Fori(0, NPAIR - 1) as bp:
                        tiles(bp * 2, bp, 0, True)
                        tiles(bp * 2 + 1, bp, 1, True)
                    tiles(NB - 2, NPAIR - 1, 0, True)
                    tiles(NB - 1, NPAIR - 1, 1, False)

                @block.scalar
                def _(act):
                    def root(call, ks=slice(0, KB)):
                        act.wait_ge(ln_ready, call * LN + 1)
                        nc.scalar.activation(sd1[:, ks], ve1[:, ks], ACT.Sqrt).then_inc(sd1_ready, 1)
                        act.wait_ge(ln_ready, (call + 1) * LN)

                    def normalise(t, p):
                        e, k = p // KB, p % KB
                        act.wait_ge(hT_ps, t + 1)
                        for h1_ in (h1[:, k % 2], h1_parts[:, k % 2, 0]):
                            last = nc.scalar.activation(h1_, x1[:, e, k], ACT.Relu, bias=nmr1[:, e, k:k + 1],
                                                        scale=rstd1[:, e, k:k + 1])
                        last.then_inc(h1_ready, 1)

                    def transposed(t, p):
                        act.wait_ge(hT_ps, t + 3)
                        act.wait_ge(both_ps, t + 1)
                        nc.scalar.activation(h1T[:, p % 2], bank16(p % 2, FP16).rearrange("p (k c) -> p k c", k=2 * FC), ACT.Copy).then_inc(hT_ready, 1)

                    def high(t, p):
                        act.wait_ge(both_ps, t + 3)
                        nc.scalar.activation(gh[:, bass.ds(t, 1)].rearrange("p o f -> p (o f)"), PS[:, 4 + p % 2, :], ACT.Copy,
                                             scale=GSCALE * UNSCALE).then_inc(gh_ready, 1)

                    def tiles(bp, last):
                        t0 = bp * PAIR
                        for p in range(PAIR):
                            if p == KB // 2 + 1:
                                root(bp * 2 + 2)
                            if p == KB + KB // 2 + 1 and not last:
                                root(bp * 2 + 3)
                            if p > 0:
                                high(t0 + p - 1, p - 1)
                            if p < PAIR - 1 or not last:
                                transposed(t0 + p + 1, p + 1)
                            if p < PAIR - 2 or not last:
                                normalise(t0 + p + 2, (p + 2) % PAIR)
                        high(t0 + PAIR - 1, PAIR - 1)

                    root(0, slice(0, KB // 2))
                    act.sem_inc(hT_ready, 2)
                    normalise(0, 0)
                    normalise(1, 1)
                    transposed(0, 0)
                    root(1, slice(KB // 2, KB))
                    with act.Fori(0, NPAIR - 1) as bp:
                        tiles(bp, False)
                    tiles(NPAIR - 1, True)

                @block.tensor
                def _(pe):
                    def transposes(t, k):
                        pe.wait_ge(h1_lo_ready, t + 1)
                        pe.wait_ge(hT_ready, t + 1)
                        for c in range(2 * FC):
                            last = nc.tensor.transpose(bank16(k % 2, FP16)[:, c * P:(c + 1) * P],
                                                       h1_parts[:, k % 2, c // FC, c % FC * P:(c % FC + 1) * P], identh[:])
                        last.then_inc(hT_ps, 1)

                    def products(t, k):
                        pe.wait_ge(hT_ready, t + 3)
                        pe.wait_ge(self_ready, t + 1)
                        pe.wait_ge(gl_ready, t + 1)
                        for i, bank in enumerate((2, 4)):
                            for c in range(FC):
                                for hp, wp in ((0, 0), (0, 1), (1, 0)):
                                    last = nc.tensor.matmul(PS[:, bank + k % 2, :], h1T[:, k % 2, hp * FC + c, :],
                                                            w_parts[:, i * FC + c, wp, :],
                                                            start=c == 0 and hp == wp, stop=c == FC - 1 and hp == 1)
                        last.then_inc(both_ps, 1)

                    pe.sem_inc(hT_ps, 2)
                    pe.sem_inc(both_ps, 2)
                    transposes(0, 0)
                    with pe.Fori(0, NB - 1) as b:
                        for k in range(KB):
                            transposes(b * KB + k + 1, k + 1)
                            products(b * KB + k, k)
                    for k in range(KB):
                        t = (NB - 1) * KB + k
                        if k < KB - 1:
                            transposes(t + 1, k + 1)
                        products(t, k)

        with ExitStack() as ctx:
            xs = sb(ctx, "xs", [P, 4, 2, F], F32)
            fin = sb(ctx, "fin", [P, 2, F], F32)
            xs_ld = [sem(f"xs_ld{i}") for i in range(TI)]
            fin_out = [sem(f"fin_out{i}") for i in range(2)]
            sum_ps, y_ready, fin_ready = (sem(n) for n in ("sum_ps", "y_ready", "fin_ready"))
            JL = 4

            with nc.Block() as block:
                @block.sync
                def _(sp):
                    load_mask(sp, m1b, 1, 1, 1)
                    with sp.Fori(0, NB1 // 2 - 1) as bp:
                        for e, m1_ in enumerate((m1a, m1b)):
                            sp.wait_ge(sum_ps, (bp * 2 + e + 1) * TI)
                            load_mask(sp, m1_, e, bp * 2 + 2 + e, bp + 2)

                @block.gpsimd
                def _(pool):
                    with pool.Fori(0, NB1) as b:
                        for ti in range(TI):
                            pool.wait_ge(fin_ready, b * TI + ti + 1)
                            pool.dma_start(xs[:, ti].rearrange("p s f -> p (s f)"),
                                           x1_self[bass.ds(b * TI + ti, 1)].rearrange("o p s f -> (o p) (s f)")).then_inc(xs_ld[ti], 16)

                @block.tensor
                def _(pe):
                    with pe.Fori(0, NB1 // 2) as bp:
                        for e, m1_ in enumerate((m1a, m1b)):
                            pe.wait_ge(m1_dg[e], (bp + 1) * 16 * TI)
                            for ti in range(TI):
                                pe.wait_ge(y_ready, (bp * 2 + e) * TI + ti + 1)

                                def tiles(j0, first, last_):
                                    for j in range(JL):
                                        for g_ in (gh, gl):
                                            ins = nc.tensor.matmul(
                                                PS[:, ti, :], m1_[:, bass.ds(j0 + j, 1), ti * P:(ti + 1) * P].rearrange("p o c -> p (o c)"),
                                                g_[:, bass.ds(j0 + j, 1), :].rearrange("p o c -> p (o c)"),
                                                start=first and j == 0 and g_ is gh, stop=last_ and j == JL - 1 and g_ is gl)
                                    return ins

                                tiles(0, True, False)
                                with pe.Fori(JL, NT - JL, JL) as j0:
                                    tiles(j0, False, False)
                                tiles(NT - JL, False, True).then_inc(sum_ps, 1)

                @block.vector
                def _(dve):
                    dve.sem_inc(fin_ready, TI)
                    dve.sem_inc(y_ready, TI)
                    with dve.Fori(0, NB1) as b:
                        for ti in range(TI):
                            t = b * TI + ti
                            dve.wait_ge(xs_ld[ti], (b + 1) * 16)
                            dve.wait_ge(fin_out[ti % 2], (b * (TI // 2) + ti // 2 + 1) * 16)
                            dve.wait_ge(sum_ps, t + 1)
                            nc.vector.scalar_tensor_tensor(out=fin[:, ti % 2], in0=PS[:, ti, :], scalar=rdeg[:, bass.ds(t, 1)],
                                                           in1=xs[:, ti, 1, :], op0=ALU.mult, op1=ALU.add).then_inc(y_ready, 1)
                            dve.wait_ge(y_ready, t + TI + 1)
                            nc.vector.scalar_tensor_tensor(out=fin[:, ti % 2], in0=fin[:, ti % 2], scalar=0.0, in1=xs[:, ti, 0, :],
                                                           op0=ALU.max, op1=ALU.add).then_inc(fin_ready, 1)

                @block.scalar
                def _(act):
                    for e in range(2):
                        act.sem_inc(fin_out[e], 16)
                    with act.Fori(0, NB1) as b:
                        for ti in range(TI):
                            t = b * TI + ti
                            act.wait_ge(fin_ready, t + TI + 1)
                            act.dma_start(out[bass.ds(t * P, P), :], fin[:, ti % 2]).then_inc(fin_out[ti % 2], 16)
                    for e in range(2):
                        act.wait_ge(fin_out[e], NT // 2 * 16 + 16)
        layer1.close()


_INS = ["x", "adj", "L0_gnn_W", "L0_gnn_a_src", "L0_gnn_a_dst", "L1_gnn_W_self", "L1_gnn_b_self",
        "L1_gnn_W_nb", "L1_gnn_b_nb", "L1_gnn_W_comb", "L1_gnn_b_comb"]


def kernel(**inputs):
    import numpy as _np
    import concourse.bacc as _bacc
    from concourse import mybir as _mybir
    from concourse.bass_utils import run_bass_kernel_spmd as _run

    nc = _bacc.Bacc("TRN2", target_bir_lowering=False, num_devices=1)
    arrays, args = {}, []
    for name in _INS:
        a = _np.ascontiguousarray(inputs[name])
        arrays[f"in_{name}_dram"] = a
        args.append(nc.dram_tensor(f"in_{name}_dram", a.shape, _mybir.dt.from_np(a.dtype), kind="ExternalInput").ap())
    out = nc.dram_tensor("out_0_dram", inputs["x"].shape, _mybir.dt.float32, kind="ExternalOutput").ap()
    build(nc, *args, out)
    r = _run(nc, [arrays], core_ids=[0])
    return r.results[0]["out_0_dram"]
```
